# Optimizing a Trainium2 kernel written in Bass

```python
import numpy as np
import jax
import jax.numpy as jnp

def _softmax(x, axis=-1):
    return jax.nn.softmax(x, axis=axis)

def _gelu(x):
    return jax.nn.gelu(x, approximate=True)

def _silu(x):
    return jax.nn.silu(x)

def _sigmoid(x):
    return jax.nn.sigmoid(x)

def _layernorm(x, axis=-1, eps=1e-05):
    m = jnp.mean(x, axis=axis, keepdims=True)
    v = jnp.var(x, axis=axis, keepdims=True)
    return (x - m) / jnp.sqrt(v + eps)

def _scatter_add(tgt, idx, src, axis=0):
    return tgt.at[idx].add(src)

def _segment_sum(src, seg, n):
    return jax.ops.segment_sum(src, seg, n)
kernel_name = 'mk_sandwich_d1_jaxref_r8_07be8e'

def setup_inputs(seed: int=0):
    np.random.seed(seed)
    _w = jnp.asarray

    def _L0_attn_setup():
        import jax, jax.numpy as jnp
        import numpy as np
        FEATURE_DIM = 16
        NUM_HEADS = 16
        HEAD_DIM = 64
        R2 = float(np.sqrt(2.0))
        RD = float(np.sqrt(FEATURE_DIM))
        RRD = float(np.sqrt(RD))
        RMS_EPS = 1e-05

        def taylor_exp(x):
            x2 = (x[..., :, None] * x[..., None, :]).reshape(*x.shape[:-1], FEATURE_DIM * FEATURE_DIM) / R2
            ones = jnp.ones_like(x[..., :1])
            return jnp.concatenate([ones, x / RRD, x2 / RD], axis=-1)

        def _reference_tuple_inner(hidden_states, Wq, Wk, Wv, Wo, g_weight):
            b, l, _ = hidden_states.shape
            q = (hidden_states @ Wq.T).reshape(b, l, NUM_HEADS, FEATURE_DIM).transpose(0, 2, 1, 3)
            k = (hidden_states @ Wk.T).reshape(b, l, NUM_HEADS, FEATURE_DIM).transpose(0, 2, 1, 3)
            v = (hidden_states @ Wv.T).reshape(b, l, NUM_HEADS, HEAD_DIM).transpose(0, 2, 1, 3)
            qf = taylor_exp(q)
            kf = taylor_exp(k)
            A_qk = jnp.einsum('bhnd,bhmd->bhnm', qf, kf)
            A_qk = jnp.tril(A_qk)
            y = jnp.einsum('bhnm,bhme->bhne', A_qk, v)
            kv_state = jnp.einsum('bhnd,bhnf->bhfd', kf, v)[:, :, None]
            rms = jax.lax.rsqrt(jnp.mean(y * y, axis=-1, keepdims=True) + RMS_EPS)
            y = y * rms * g_weight
            y = y.transpose(0, 2, 1, 3).reshape(b, l, NUM_HEADS * HEAD_DIM)
            out = y @ Wo.T
            return (out, kv_state)
        key = jax.random.key(seed)
        ks = jax.random.split(key, 5)
        b, l, d_model = (4, 256, 128)
        inp = {'hidden_states': jax.random.normal(ks[0], (b, l, d_model), dtype=jnp.float32), 'Wq': jax.random.normal(ks[1], (FEATURE_DIM * NUM_HEADS, d_model), dtype=jnp.float32) * 0.02, 'Wk': jax.random.normal(ks[2], (FEATURE_DIM * NUM_HEADS, d_model), dtype=jnp.float32) * 0.02, 'Wv': jax.random.normal(ks[3], (NUM_HEADS * HEAD_DIM, d_model), dtype=jnp.float32) * 0.02, 'Wo': jax.random.normal(ks[4], (d_model, NUM_HEADS * HEAD_DIM), dtype=jnp.float32) * 0.02, 'g_weight': jnp.ones((HEAD_DIM,), dtype=jnp.float32)}
        return inp
    _L0_attn_in = _L0_attn_setup()

    def _L0_ffn_setup():
        import jax, jax.numpy as jnp
        import numpy as np
        DIM = 128
        DEPTH = 6
        HEADS = 16
        DIM_HEAD = 64
        WINDOW = 32
        INNER = HEADS * DIM_HEAD
        DIM_INNER = int(DIM * 4 * 2 / 3)
        QK_SCALE = 8.0

        def shift_tokens(t):
            a, s = jnp.split(t, 2, -1)
            s = jnp.pad(s, ((0, 0), (1, 0), (0, 0)))[:, :-1]
            return jnp.concatenate([a, s], -1)

        def l2norm(t):
            return t / jnp.maximum(jnp.linalg.norm(t, axis=-1, keepdims=True), 1e-12)

        def rotate_half(x):
            x1, x2 = jnp.split(x, 2, -1)
            return jnp.concatenate([-x2, x1], -1)

        def rotary_tables(n):
            half = jnp.arange(0, DIM_HEAD, 2, dtype=jnp.float32)
            inv_freq = 1.0 / 10000.0 ** (half / DIM_HEAD)
            t = jnp.arange(n, dtype=jnp.float32)
            freqs = t[:, None] * inv_freq[None, :]
            freqs = jnp.concatenate([freqs, freqs], -1)
            base_scale = (half + 0.4 * DIM_HEAD) / (1.4 * DIM_HEAD)
            power = (t - n // 2) / (WINDOW // 2)
            scale = base_scale[None, :] ** power[:, None]
            scale = jnp.concatenate([scale, scale], -1)
            return (freqs, scale)

        def local_attention(q, k, v):
            b, h, n, d = q.shape
            w = WINDOW
            nw = n // w
            bq = q.reshape(b, h, nw, w, d)
            bk = k.reshape(b, h, nw, w, d)
            bv = v.reshape(b, h, nw, w, d)

            def look(t):
                p = jnp.pad(t, ((0, 0), (0, 0), (1, 0), (0, 0), (0, 0)))
                return jnp.concatenate([p[:, :, :nw], p[:, :, 1:]], axis=3)
            bk2, bv2 = (look(bk), look(bv))
            seq = jnp.arange(n).reshape(nw, w)
            seq_p = jnp.pad(seq, ((1, 0), (0, 0)), constant_values=-1)
            jt = jnp.concatenate([seq_p[:nw], seq_p[1:]], axis=1)
            it = seq[:, :, None]
            jb = jt[:, None, :]
            mask = (it < jb) | (it > jb + w) | (jb == -1)
            sim = jnp.einsum('bhwie,bhwje->bhwij', bq, bk2) * QK_SCALE
            sim = jnp.where(mask, -jnp.finfo(sim.dtype).max, sim)
            attn = jax.nn.softmax(sim, -1)
            out = jnp.einsum('bhwij,bhwje->bhwie', attn, bv2)
            return out.reshape(b, h, n, d)

        def attn_layer(x, Wqkv, qs, ksc, Wo):
            b, n, _ = x.shape
            qkv = x @ Wqkv
            q, k, v = jnp.split(qkv, 3, -1)
            sh = lambda t: t.reshape(b, n, HEADS, DIM_HEAD).transpose(0, 2, 1, 3)
            q, k, v = (sh(q), sh(k), sh(v))
            q = l2norm(q) * qs
            k = l2norm(k) * ksc
            freqs, scale = rotary_tables(n)
            cos, sin = (jnp.cos(freqs), jnp.sin(freqs))
            q = q * cos * scale + rotate_half(q) * sin * scale
            inv = 1.0 / scale
            k = k * cos * inv + rotate_half(k) * sin * inv
            out = local_attention(q, k, v)
            out = out.transpose(0, 2, 1, 3).reshape(b, n, INNER)
            return out @ Wo

        def ffn_layer(x, g, bln, W1, b1, W2, b2):
            mu = x.mean(-1, keepdims=True)
            var = ((x - mu) ** 2).mean(-1, keepdims=True)
            xn = (x - mu) / jnp.sqrt(var + 1e-05) * g + bln
            hg = xn @ W1 + b1
            a, gate = jnp.split(hg, 2, -1)
            return a * jax.nn.gelu(gate, approximate=False) @ W2 + b2
        key = jax.random.key(seed)
        ks = jax.random.split(key, 8)
        B, N = (2, 256)
        init = lambda k, shape: jax.random.normal(k, shape, jnp.float32) * 0.02
        return {'x': jax.random.normal(ks[0], (B, N, DIM), jnp.float32), 'Wqkv': init(ks[1], (DEPTH, DIM, 3 * INNER)), 'q_scale': jnp.ones((DEPTH, DIM_HEAD), jnp.float32), 'k_scale': jnp.ones((DEPTH, DIM_HEAD), jnp.float32), 'Wo': init(ks[2], (DEPTH, INNER, DIM)), 'ln_g': jnp.ones((DEPTH, DIM), jnp.float32), 'ln_b': jnp.zeros((DEPTH, DIM), jnp.float32), 'W1': init(ks[3], (DEPTH, DIM, 2 * DIM_INNER)), 'b1': jnp.zeros((DEPTH, 2 * DIM_INNER), jnp.float32), 'W2': init(ks[4], (DEPTH, DIM_INNER, DIM)), 'b2': jnp.zeros((DEPTH, DIM), jnp.float32)}
    _L0_ffn_in = _L0_ffn_setup()
    _d = {'L0_attn_hidden_states': _L0_attn_in['hidden_states'], 'L0_attn_Wq': _L0_attn_in['Wq'], 'L0_attn_Wk': _L0_attn_in['Wk'], 'L0_attn_Wv': _L0_attn_in['Wv'], 'L0_attn_Wo': _L0_attn_in['Wo'], 'L0_attn_g_weight': _L0_attn_in['g_weight'], 'L0_ffn_Wqkv': _L0_ffn_in['Wqkv'], 'L0_ffn_q_scale': _L0_ffn_in['q_scale'], 'L0_ffn_k_scale': _L0_ffn_in['k_scale'], 'L0_ffn_Wo': _L0_ffn_in['Wo'], 'L0_ffn_ln_g': _L0_ffn_in['ln_g'], 'L0_ffn_ln_b': _L0_ffn_in['ln_b'], 'L0_ffn_W1': _L0_ffn_in['W1'], 'L0_ffn_b1': _L0_ffn_in['b1'], 'L0_ffn_W2': _L0_ffn_in['W2'], 'L0_ffn_b2': _L0_ffn_in['b2']}
    _x0 = _d['L0_attn_hidden_states']
    _d['L0_attn_hidden_states'] = jax.random.normal(jax.random.fold_in(jax.random.key(seed), 1), (8, 512, 128), dtype=_x0.dtype)
    del _x0
    return _d

def reference(L0_attn_hidden_states, L0_attn_Wq, L0_attn_Wk, L0_attn_Wv, L0_attn_Wo, L0_attn_g_weight, L0_ffn_Wqkv, L0_ffn_q_scale, L0_ffn_k_scale, L0_ffn_Wo, L0_ffn_ln_g, L0_ffn_ln_b, L0_ffn_W1, L0_ffn_b1, L0_ffn_W2, L0_ffn_b2):

    def _L0_attn_ref(hidden_states, Wq, Wk, Wv, Wo, g_weight):
        import jax, jax.numpy as jnp
        import numpy as np
        FEATURE_DIM = 16
        NUM_HEADS = 16
        HEAD_DIM = 64
        R2 = float(np.sqrt(2.0))
        RD = float(np.sqrt(FEATURE_DIM))
        RRD = float(np.sqrt(RD))
        RMS_EPS = 1e-05

        def taylor_exp(x):
            x2 = (x[..., :, None] * x[..., None, :]).reshape(*x.shape[:-1], FEATURE_DIM * FEATURE_DIM) / R2
            ones = jnp.ones_like(x[..., :1])
            return jnp.concatenate([ones, x / RRD, x2 / RD], axis=-1)

        def _reference_tuple_inner(hidden_states, Wq, Wk, Wv, Wo, g_weight):
            b, l, _ = hidden_states.shape
            q = (hidden_states @ Wq.T).reshape(b, l, NUM_HEADS, FEATURE_DIM).transpose(0, 2, 1, 3)
            k = (hidden_states @ Wk.T).reshape(b, l, NUM_HEADS, FEATURE_DIM).transpose(0, 2, 1, 3)
            v = (hidden_states @ Wv.T).reshape(b, l, NUM_HEADS, HEAD_DIM).transpose(0, 2, 1, 3)
            qf = taylor_exp(q)
            kf = taylor_exp(k)
            A_qk = jnp.einsum('bhnd,bhmd->bhnm', qf, kf)
            A_qk = jnp.tril(A_qk)
            y = jnp.einsum('bhnm,bhme->bhne', A_qk, v)
            kv_state = jnp.einsum('bhnd,bhnf->bhfd', kf, v)[:, :, None]
            rms = jax.lax.rsqrt(jnp.mean(y * y, axis=-1, keepdims=True) + RMS_EPS)
            y = y * rms * g_weight
            y = y.transpose(0, 2, 1, 3).reshape(b, l, NUM_HEADS * HEAD_DIM)
            out = y @ Wo.T
            return (out, kv_state)
        return _reference_tuple_inner(hidden_states, Wq, Wk, Wv, Wo, g_weight)[0]

    def _L0_ffn_ref(x, Wqkv, q_scale, k_scale, Wo, ln_g, ln_b, W1, b1, W2, b2):
        import jax, jax.numpy as jnp
        import numpy as np
        DIM = 128
        DEPTH = 6
        HEADS = 16
        DIM_HEAD = 64
        WINDOW = 32
        INNER = HEADS * DIM_HEAD
        DIM_INNER = int(DIM * 4 * 2 / 3)
        QK_SCALE = 8.0

        def shift_tokens(t):
            a, s = jnp.split(t, 2, -1)
            s = jnp.pad(s, ((0, 0), (1, 0), (0, 0)))[:, :-1]
            return jnp.concatenate([a, s], -1)

        def l2norm(t):
            return t / jnp.maximum(jnp.linalg.norm(t, axis=-1, keepdims=True), 1e-12)

        def rotate_half(x):
            x1, x2 = jnp.split(x, 2, -1)
            return jnp.concatenate([-x2, x1], -1)

        def rotary_tables(n):
            half = jnp.arange(0, DIM_HEAD, 2, dtype=jnp.float32)
            inv_freq = 1.0 / 10000.0 ** (half / DIM_HEAD)
            t = jnp.arange(n, dtype=jnp.float32)
            freqs = t[:, None] * inv_freq[None, :]
            freqs = jnp.concatenate([freqs, freqs], -1)
            base_scale = (half + 0.4 * DIM_HEAD) / (1.4 * DIM_HEAD)
            power = (t - n // 2) / (WINDOW // 2)
            scale = base_scale[None, :] ** power[:, None]
            scale = jnp.concatenate([scale, scale], -1)
            return (freqs, scale)

        def local_attention(q, k, v):
            b, h, n, d = q.shape
            w = WINDOW
            nw = n // w
            bq = q.reshape(b, h, nw, w, d)
            bk = k.reshape(b, h, nw, w, d)
            bv = v.reshape(b, h, nw, w, d)

            def look(t):
                p = jnp.pad(t, ((0, 0), (0, 0), (1, 0), (0, 0), (0, 0)))
                return jnp.concatenate([p[:, :, :nw], p[:, :, 1:]], axis=3)
            bk2, bv2 = (look(bk), look(bv))
            seq = jnp.arange(n).reshape(nw, w)
            seq_p = jnp.pad(seq, ((1, 0), (0, 0)), constant_values=-1)
            jt = jnp.concatenate([seq_p[:nw], seq_p[1:]], axis=1)
            it = seq[:, :, None]
            jb = jt[:, None, :]
            mask = (it < jb) | (it > jb + w) | (jb == -1)
            sim = jnp.einsum('bhwie,bhwje->bhwij', bq, bk2) * QK_SCALE
            sim = jnp.where(mask, -jnp.finfo(sim.dtype).max, sim)
            attn = jax.nn.softmax(sim, -1)
            out = jnp.einsum('bhwij,bhwje->bhwie', attn, bv2)
            return out.reshape(b, h, n, d)

        def attn_layer(x, Wqkv, qs, ksc, Wo):
            b, n, _ = x.shape
            qkv = x @ Wqkv
            q, k, v = jnp.split(qkv, 3, -1)
            sh = lambda t: t.reshape(b, n, HEADS, DIM_HEAD).transpose(0, 2, 1, 3)
            q, k, v = (sh(q), sh(k), sh(v))
            q = l2norm(q) * qs
            k = l2norm(k) * ksc
            freqs, scale = rotary_tables(n)
            cos, sin = (jnp.cos(freqs), jnp.sin(freqs))
            q = q * cos * scale + rotate_half(q) * sin * scale
            inv = 1.0 / scale
            k = k * cos * inv + rotate_half(k) * sin * inv
            out = local_attention(q, k, v)
            out = out.transpose(0, 2, 1, 3).reshape(b, n, INNER)
            return out @ Wo

        def ffn_layer(x, g, bln, W1, b1, W2, b2):
            mu = x.mean(-1, keepdims=True)
            var = ((x - mu) ** 2).mean(-1, keepdims=True)
            xn = (x - mu) / jnp.sqrt(var + 1e-05) * g + bln
            hg = xn @ W1 + b1
            a, gate = jnp.split(hg, 2, -1)
            return a * jax.nn.gelu(gate, approximate=False) @ W2 + b2
        for i in range(DEPTH):
            x = attn_layer(shift_tokens(x), Wqkv[i], q_scale[i], k_scale[i], Wo[i]) + x
            x = ffn_layer(shift_tokens(x), ln_g[i], ln_b[i], W1[i], b1[i], W2[i], b2[i]) + x
        return x
    x = L0_attn_hidden_states
    x = x + _layernorm(_L0_attn_ref(_layernorm(x, axis=-1), L0_attn_Wq, L0_attn_Wk, L0_attn_Wv, L0_attn_Wo, L0_attn_g_weight), axis=-1)
    x = x + _layernorm(_L0_ffn_ref(_layernorm(x, axis=-1), L0_ffn_Wqkv, L0_ffn_q_scale, L0_ffn_k_scale, L0_ffn_Wo, L0_ffn_ln_g, L0_ffn_ln_b, L0_ffn_W1, L0_ffn_b1, L0_ffn_W2, L0_ffn_b2), axis=-1)
    return x

_drawn_inputs = setup_inputs


def setup_inputs(seed=0):
    import zlib

    import numpy as np

    out = dict(_drawn_inputs(seed))
    spreads = {'L0_attn_g_weight': (1.0, 0.2),
     'L0_ffn_q_scale': (1.0, 0.6),
     'L0_ffn_k_scale': (1.0, 0.6),
     'L0_ffn_ln_g': (1.0, 0.6),
     'L0_ffn_ln_b': (0.0, 0.8),
     'L0_ffn_b1': (0.0, 0.8),
     'L0_ffn_b2': (0.0, 0.338)}
    factors = {'L0_ffn_W1': 4.556, 'L0_ffn_W2': 4.467}
    for name, (base, spread) in spreads.items():
        noise = np.random.default_rng([zlib.crc32(name.encode()), seed]).standard_normal(out[name].shape)
        drawn = base * np.exp(spread * noise) if base else spread * noise
        out[name] = jnp.asarray(drawn.astype(out[name].dtype))
    for name, factor in factors.items():
        out[name] = (out[name] * factor).astype(out[name].dtype)
    return out
```

```python
from contextlib import ExitStack

import numpy as np
import concourse.bass as bass
from concourse import mybir

F32 = mybir.dt.float32
F32R = mybir.dt.float32r
BF16 = mybir.dt.bfloat16
ACT = mybir.ActivationFunctionType
ALU = mybir.AluOpType
AX_X = mybir.AxisListType.X

NB, L, D = 8, 512, 128
DEPTH = 6
F1 = 341
FP = [(0, 114), (114, 114), (228, 113)]
EPS = 1e-5
NEG = -1.0e30
QB = [(96 * t, min(96, L - 96 * t)) for t in range(6)]

CONST = {}
CONST_COLS = 0
for _n, _w in (("ident", 128), ("cm", 128), ("om", 128), ("bd", 128), ("ones", 128), ("tri", 128), ("hsel", 2),
               ("cum", 12), ("mske", 16), ("half", 2), ("nsel", 256), ("bsel", 1024), ("tab", 2048), ("mask", 512)):
    CONST[_n] = (CONST_COLS, _w)
    CONST_COLS += _w


def constants():
    c = np.zeros((128, CONST_COLS), np.float32)

    def part(n):
        o, w = CONST[n]
        return c[:, o:o + w]

    eye = np.eye(128, dtype=np.float32)
    part("ident")[:] = eye
    part("cm")[:] = eye - np.float32(1.0 / 128)
    part("om")[:] = 1.0 / 128
    r = np.arange(128)
    part("bd")[:] = (r[:, None] // 64 == r[None, :] // 64) / 64.0
    part("ones")[:] = 1.0
    part("tri")[:] = r[:, None] <= r[None, :]
    part("hsel")[:] = r[:, None] // 64 == np.arange(2)[None, :]
    for j in range(3):
        for i in range(4):
            part("cum")[:, 4 * j + i] = float(i > j)
    for p in range(32):
        part("mske")[p, p % 16] = 1.0
        part("nsel")[p, 128 * (p // 16):128 * (p // 16) + 128] = -1.0
    part("half")[:, 0] = -0.5
    for i in range(8):
        for s in range(2):
            for base in (0, 32):
                part("bsel")[base + 2 * i + s, 128 * i + 64 * s:128 * i + 64 * s + 64] = 1.0
    half = np.arange(0, 64, 2, dtype=np.float32)
    inv_freq = (1.0 / np.float32(10000.0) ** (half / np.float32(64))).astype(np.float32)
    t = np.arange(L, dtype=np.float32)
    freqs = (t[:, None] * inv_freq[None, :]).astype(np.float32)
    base = ((half + 0.4 * 64) / (1.4 * 64)).astype(np.float64)
    power = (np.arange(L) - L // 2) / 16.0
    scale = base[None, :] ** power[:, None]
    cos, sin = np.cos(freqs.astype(np.float64)), np.sin(freqs.astype(np.float64))
    sgn = np.where(np.arange(64) < 32, -1.0, 1.0)

    def dims(a):
        return np.concatenate([a, a], 1)

    tabs = [dims(cos * scale) * 8.0, dims(sin * scale) * sgn * 8.0, dims(cos / scale), dims(sin / scale) * sgn]
    for i, a in enumerate(tabs):
        part("tab")[:, 512 * i:512 * i + 512] = np.concatenate([a.T, a.T], 0)
    m = np.full((128, L), NEG, np.float32)
    for ti, (q0, nq) in enumerate(QB):
        for q in range(q0, q0 + nq):
            for rr in range(128):
                j = q0 - 32 + rr
                if 0 <= j < L and 0 <= q - j <= 32:
                    m[rr, q] = 0.0
    part("mask")[:] = m
    return c


class Tok:

    def __init__(self, eng):
        self.eng, self.used, self.sem, self.val = eng, False, None, 0


class Queues:

    def __init__(self):
        self.q = {e: [] for e in ("pe", "act", "dve", "pool", "sp")}
        self.phase = 0

    def op(self, eng, fn, *after, sem=None):
        tok = Tok(eng)
        flat = []
        for a in after:
            flat += a if isinstance(a, list) else [a]
        flat = [a for a in flat if a is not None]
        for a in flat:
            a.used = True
        self.q[eng].append((fn, flat, tok, sem, self.phase))
        return tok

    def number(self, new_sem):
        sems, counts = {}, {}
        for eng, ops in self.q.items():
            for fn, after, tok, sem, phase in ops:
                if sem is None and not tok.used:
                    continue
                key = sem if sem is not None else (eng, phase)
                if key not in sems:
                    sems[key] = new_sem("s_" + "_".join(str(x) for x in (key if isinstance(key, tuple) else (key,))))
                    counts[key] = 0
                counts[key] += 16 if sem is not None else 1
                tok.sem, tok.val = sems[key], counts[key]
                tok.key = key

    def emit(self, eng, e):
        seen = {}
        for fn, after, tok, sem, phase in self.q[eng]:
            for a in after:
                if seen.get(a.key, 0) < a.val:
                    e.wait_ge(a.sem, a.val)
                    seen[a.key] = a.val
            if fn is None:
                continue
            ins = fn(e)
            if tok.sem is not None:
                ins.then_inc(tok.sem, 16 if sem is not None else 1)


class Slot:

    def __init__(self, buf, ring=None):
        self.buf, self.ring, self.after = buf, ring, []

    @property
    def free(self):
        return self.after

    @free.setter
    def free(self, toks):
        self.after = toks
        if self.ring is not None:
            assert self not in self.ring, "given back twice"
            self.ring.append(self)


class Ring:

    def __init__(self, bufs):
        self.idle = []
        self.idle += [Slot(b, self.idle) for b in bufs]

    def take(self):
        assert self.idle, "every buffer is in use"
        s = self.idle.pop(0)
        return s, s.after


def i_activation(*a, **k):
    return lambda e: e.activation(*a, **k)


def i_copy(*a, **k):
    return lambda e: e.copy(*a, **k)


def i_memset(*a, **k):
    return lambda e: e.memset(*a, **k)


def i_reciprocal(*a, **k):
    return lambda e: e.reciprocal(*a, **k)


def i_scalar_tensor_tensor(*a, **k):
    return lambda e: e.scalar_tensor_tensor(*a, **k)


def i_tensor_copy(*a, **k):
    return lambda e: e.tensor_copy(*a, **k)


def i_tensor_reduce(*a, **k):
    return lambda e: e.tensor_reduce(*a, **k)


def i_tensor_scalar(*a, **k):
    return lambda e: e.tensor_scalar(*a, **k)


def i_tensor_tensor(*a, **k):
    return lambda e: e.tensor_tensor(*a, **k)


def i_transpose(*a, **k):
    return lambda e: e.transpose(*a, **k)


def build(nc, xin, cst, awq, awk, awv, awo, wqkv, wo, w1, w2, vec, out):
    with ExitStack() as ctx:
        def sb(name, shape, dt=F32):
            return ctx.enter_context(nc.sbuf_tensor(name, shape, dt))

        x1d = nc.dram_tensor("x1_scratch", (128, NB, L), F32, kind="Internal").ap()
        bank = [ctx.enter_context(nc.psum_tensor(f"bank{i}", [128, 512], F32)) for i in range(8)]
        X = sb("X", [128, NB, L + 33])
        C = sb("C", [128, CONST_COLS])
        WQ = sb("WQ", [128, 3072])
        WR = sb("WR", [128, 2048])
        WO = sb("WO", [128, 8, 128])
        W1 = sb("W1", [128, 2 * F1])
        W2 = sb("W2", [128, 3, 128])
        VEC = sb("VEC", [128, DEPTH, 16])
        TAB = sb("TAB", [128, 4, L])
        Q = sb("Q", [128, 8, L])
        K = sb("K", [128, 8, L + 32])
        V = sb("V", [128, 6, 1024])
        AO = sb("AO", [128, 8, L])
        SQ = sb("SQ", [128, 8, L])
        nselr = sb("nselr", [32, 256], F32R)
        bselr = sb("bselr", [64, 1024], F32R)
        identb = sb("identb", [128, 128], BF16)
        maskb = sb("maskb", [128, L], BF16)
        R = sb("R", [64, L], F32R)
        ssb = sb("ssb", [128, 64])
        rsb = sb("rsb", [128, 64])
        cumt = sb("cumt", [128, 32])
        Tr = Ring([sb(f"T{i}", [128, L]) for i in range(9)])
        Er = Ring([sb(f"E{i}", [32, L], F32R) for i in range(2)])
        Pr = Ring([sb(f"P{i}", [128, L]) for i in range(4)])
        Mr = Ring([sb(f"M{i}", [128, 64]) for i in range(3)])
        G = Ring(bank[0:3])
        S = Ring(bank[3:6])
        yb, sb_bank = Slot(bank[6]), Slot(bank[7])

        def cn(n, rows=128):
            o, w = CONST[n]
            return C[0:rows, o:o + w]

        q = Queues()
        op = q.op

        def pe(fn, *a):
            return op("pe", fn, *a)

        def act(fn, *a):
            return op("act", fn, *a)

        def dve(fn, *a):
            return op("dve", fn, *a)

        def pool(fn, *a):
            return op("pool", fn, *a)

        def dma(o, i, key, *a):
            return op("sp", lambda e, o=o, i=i: e.dma_start(o, i), *a, sem=key)

        def mm(o, lhsT, rhs, start=True, stop=True, **kw):
            return lambda e: e.matmul(o, lhsT, rhs, start=start, stop=stop, **kw)

        t_c = dma(C[:, :], cst, "c")
        t_v = dma(VEC[:, :, :], vec, "v")
        z0 = pool(i_memset(X[:, :, 0:33], 0.0))
        z1 = pool(i_memset(K[:, :, 0:32], 0.0))
        z2 = pool(i_memset(WQ[:, 0:1024], 0.0))
        c1 = dve(i_tensor_copy(nselr[:, :], cn("nsel", 32)), t_c)
        c2 = dve(i_tensor_copy(bselr[:, :], cn("bsel", 64)), t_c)
        c3 = dve(i_tensor_copy(identb[:, :], cn("ident")), t_c)
        c4 = dve(i_tensor_copy(maskb[:, :], cn("mask")), t_c)
        c5 = dve(i_tensor_scalar(R[:, :], cn("mask", 64), 0.0, None, ALU.mult), t_c)
        t_aq = dma(WQ[:, 0:512].rearrange("p (h c) -> p h c", c=32)[:, :, 0:16],
                   awq.rearrange("p (h c) -> p h c", c=16), "w0", z2)
        t_ak = dma(WQ[:, 512:1024].rearrange("p (h c) -> p h c", c=32)[:, :, 0:16],
                   awk.rearrange("p (h c) -> p h c", c=16), "w1", z2)
        t_av = dma(WQ[:, 1024:2048], awv, "w2")
        t_ao = dma(WO[:, :, :], awo.rearrange("p (c d) -> p c d", c=8), "w3")
        ident = cn("ident")
        mhalf = cn("half")[:, 0:1]

        def power(dst, src, n, *a):
            return pool(i_tensor_tensor(dst, src, mhalf.broadcast_to([128, n]), ALU.pow), *a)

        def norm(src, srcs):
            g, f = G.take()
            last = None
            for i, (lhs, rhs) in enumerate(src):
                last = pe(mm(g.buf[:, :], lhs, rhs, i == 0, i == len(src) - 1), *srcs, *f, t_c)
            s1, f1 = Tr.take()
            a = act(i_activation(s1.buf[:, :], g.buf[:, :], ACT.Square), last, *f1)
            s2, f2 = Tr.take()
            d = dve(i_tensor_copy(s2.buf[:, :], g.buf[:, :]), a, *f2)
            g.free = [d]
            yield
            g2, f = G.take()
            p = pe(mm(g2.buf[:, :], cn("om"), s1.buf[:, :]), a, *f)
            d2 = dve(i_tensor_scalar(s1.buf[:, :], g2.buf[:, :], EPS, None, ALU.add), p)
            g2.free = [d2]
            yield
            d3 = power(s1.buf[:, :], s1.buf[:, :], L, d2)
            return s2, d, s1, d3

        x_ready = [None] * NB
        x1_store = [None] * NB
        a_state = {"q": None, "v": None, "ao": None}
        cmt = cn("cm")

        def part_a(b):
            s0, f = Tr.take()
            t_x = dma(s0.buf[:, :].rearrange("p (a d) -> p a d", a=4), xin[b].rearrange("(a p) d -> p a d", p=128),
                      f"x{b % 2}", *f)
            g, f = G.take()
            for i in range(4):
                p = pe(i_transpose(g.buf[:, 128 * i:128 * i + 128], s0.buf[:, 128 * i:128 * i + 128], ident),
                       t_x, t_c, *f)
            xa, f = Tr.take()
            s0.free = [p]
            t_xa = act(i_copy(xa.buf[:, :], g.buf[:, :]), p, *f)
            g.free = [t_xa]
            yield
            xc, d, rr, d3 = yield from norm([(cmt, xa.buf[:, :])], [t_xa])
            yield
            xn, f = Tr.take()
            t_xn = dve(i_tensor_tensor(xn.buf[:, :], xc.buf[:, :], rr.buf[:, :], ALU.mult), d, d3, *f)
            xc.free = [t_xn]
            rr.free = [t_xn]
            t_qk = []
            for n, wt in ((0, t_aq), (1, t_ak)):
                for i in range(4):
                    g, f = G.take()
                    p = pe(mm(g.buf[:, :], WQ[:, 512 * n + 128 * i:512 * n + 128 * i + 128], xn.buf[:, :]), t_xn, wt, *f)
                    t = act(i_copy(Q[:, 4 * n + i, :], g.buf[:, :]), p, a_state["q"])
                    g.free = [t]
                    t_qk.append(t)
                yield
            t_vv = []
            for i in range(4):
                for n in range(2):
                    g, f = G.take()
                    p = pe(mm(g.buf[:, :], xn.buf[:, 128 * i:128 * i + 128], WQ[:, 1024 + 512 * n:1536 + 512 * n]), t_av, *f)
                    t = dve(i_tensor_copy(V[:, i, 512 * n:512 * n + 512], g.buf[:, :]), p, a_state["v"])
                    g.free = [t]
                    t_vv.append(t)
                yield
            xn.free = [p]
            g, f = G.take()
            for h in range(8):
                for j in range(3):
                    p = pe(mm(g.buf[:, 4 * h:4 * h + 4], V[:, j, 128 * h:128 * h + 128], cn("cum")[:, 4 * j:4 * j + 4],
                              h == 0 and j == 0, h == 7 and j == 2, skip_group_check=True), t_vv, *f)
            t_cum = dve(i_tensor_copy(cumt[:, :], g.buf[:, 0:32]), p, a_state.get("cum"))
            g.free = [t_cum]
            yield
            t_y = []
            for hp in range(8):
                f_y = yb.free if hp % 2 == 0 else sb_bank.free
                ybank = yb if hp % 2 == 0 else sb_bank
                for j in range(4):
                    pts = []
                    n = L - 128 * j
                    for s in range(2):
                        h = 2 * hp + s
                        r0 = 32 * (h % 4)
                        st, f = S.take()
                        p = pe(mm(st.buf[:, 0:n], Q[r0:r0 + 16, 4 + h // 4, 128 * j:128 * j + 128],
                                  Q[r0:r0 + 16, h // 4, 128 * j:512]), t_qk, *f)
                        pt, f = Pr.take()
                        t = act(i_activation(pt.buf[:, 0:n], st.buf[:, 0:n], ACT.Square,
                                                                         bias=1.0, scale=0.25), p, *f)
                        st.free = [t]
                        t2 = dve(i_scalar_tensor_tensor(pt.buf[:, 0:128], pt.buf[:, 0:128], 1.0, cn("tri"),
                                                                         ALU.add, ALU.mult), t)
                        pts.append((pt, [t, t2]))
                    for s in range(2):
                        h = 2 * hp + s
                        pt, tt = pts[s]
                        p2 = pe(mm(ybank.buf[64 * s:64 * s + 64, 128 * j:512], V[:, j, 64 * h:64 * h + 64], pt.buf[:, 0:n],
                                   j == 0, j == 3), tt, f_y)
                        pt.free = [p2]
                    yield
                y, f = Tr.take()
                cb = cumt[:, 4 * hp:4 * hp + 4].rearrange("p (a o) -> p a o", o=1).broadcast_to([128, 4, 128])
                d = dve(i_tensor_tensor(
                    y.buf[:, :].rearrange("p (a c) -> p a c", a=4), ybank.buf[:, :].rearrange("p (a c) -> p a c", a=4), cb, ALU.add),
                    p2, t_cum, *f)
                ybank.free = [d]
                sq, f = Tr.take()
                a = act(i_activation(sq.buf[:, :], y.buf[:, :], ACT.Square), d, *f)
                g, f = G.take()
                p = pe(mm(g.buf[:, :], cn("bd"), sq.buf[:, :]), a, *f)
                d2 = dve(i_tensor_scalar(sq.buf[:, :], g.buf[:, :], 4 * EPS, None, ALU.add), p)
                g.free = [d2]
                d3 = power(sq.buf[:, :], sq.buf[:, :], L, d2)
                d4 = dve(i_scalar_tensor_tensor(
                    AO[:, hp, :], y.buf[:, :], VEC[:, 0, 13:14], sq.buf[:, :], ALU.mult, ALU.mult), d3, d, t_v, a_state["ao"])
                y.free = [d4]
                sq.free = [d4]
                t_y.append(d4)
            a_state["q"] = a_state["v"] = p2
            a_state["cum"] = d
            g, f = G.take()
            for i in range(8):
                p = pe(mm(g.buf[:, :], WO[:, i, :], AO[:, i, :], i == 0, i == 7), t_y, t_ao, *f)
            a_state["ao"] = p
            z, f = Tr.take()
            t_z = act(i_copy(z.buf[:, :], g.buf[:, :]), p, *f)
            g.free = [t_z]
            yield
            xc, d, rr, d3 = yield from norm([(cmt, z.buf[:, :])], [t_z])
            m = dve(i_tensor_tensor(z.buf[:, :], xc.buf[:, :], rr.buf[:, :], ALU.mult), d, d3)
            xc.free = [m]
            rr.free = [m]
            t_x1 = pool(i_tensor_tensor(xa.buf[:, :], xa.buf[:, :], z.buf[:, :], ALU.add), m, t_xa)
            x1_store[b] = dma(x1d[:, b, :], xa.buf[:, :], f"x1s{b}", t_x1)
            z.free = [t_x1]
            yield
            xc, d, rr, d3 = yield from norm([(cmt, xa.buf[:, :])], [t_x1])
            xa.free = [x1_store[b], d]
            m1 = dve(i_tensor_tensor(X[0:64, b, 32:32 + L], xc.buf[0:64, :], rr.buf[0:64, :], ALU.mult), d, d3, z0)
            m2 = dve(i_tensor_tensor(X[64:128, b, 33:33 + L], xc.buf[64:128, :], rr.buf[64:128, :], ALU.mult), d, d3, z0)
            xc.free = [m1, m2]
            rr.free = [m1, m2]
            x_ready[b] = [m1, m2]
            a_state["end"] = p
            yield

        def run(*gens):
            gens = list(gens)
            while gens:
                for g in list(gens):
                    try:
                        next(g)
                    except StopIteration:
                        gens.remove(g)

        def steps(g, n=1):
            for _ in range(n):
                try:
                    next(g)
                except StopIteration:
                    return False
            return True

        for b in range(NB):
            run(part_a(b))
        end_a = a_state["end"]

        wq_done, wo_done, w12_done, tab_done = [end_a], [a_state["ao"]], [], []
        st = {"k": {}, "v": None, "ao": None}
        for hp in range(8):
            st["k"][hp] = None
        for layer in range(DEPTH):
            q.phase += 1
            t_wq = dma(WQ[:, :], wqkv[layer], "w4", wq_done)
            t_wo = dma(WO[:, :, :], wo[layer].rearrange("(c p) d -> p c d", p=128), "w5", wo_done)
            t_w1 = dma(W1[:, :], w1[layer], "w6", w12_done)
            t_w2 = [dma(W2[0:n, i, :], w2[layer, o:o + n, :], f"w{7 + i}", w12_done) for i, (o, n) in enumerate(FP)]
            t_tab = []
            tb = CONST["tab"][0]
            for i in range(4):
                t_tab.append(pool(i_tensor_scalar(
                    TAB[:, i, :], C[:, tb + 512 * i:tb + 512 * i + 512], VEC[:, layer, 9 + i:10 + i], None, ALU.mult),
                    t_c, t_v, tab_done))
            t_wr = []
            for i in range(4):
                c = 512 * i
                t_wr.append(pool(i_tensor_copy(
                    WR[:, c:c + 512].rearrange("p (h a c) -> p h a c", a=2, c=32),
                    WQ[:, c:c + 512].rearrange("p (h a c) -> p h a c", a=2, c=32)[:, :, ::-1, :]), t_wq, wq_done))
            v_ready = {}
            qk_ready = {}
            wq_reads = []

            def vproj(b):
                toks = []
                for t in range(6):
                    n = 128 if t < 5 else 64
                    for c in range(2):
                        g, f = G.take()
                        p = pe(mm(g.buf[0:n, :], X[:, b, 96 * t:96 * t + n], WQ[:, 2048 + 512 * c:2560 + 512 * c]),
                               t_wq, x_ready[b], *f)
                        a = act(i_copy(V[0:n, t, 512 * c:512 * c + 512], g.buf[0:n, :]),
                                p, st["v"])
                        g.free = [a]
                        toks.append(a)
                    yield
                v_ready[b] = toks
                wq_reads.append(p)

            def proj(b, hf):
                src = X[:, b, 32:32 + L]
                sqt = []
                raw = []
                for i in range(4):
                    hp = 4 * hf + i
                    for w in range(2):
                        wcol = WQ[:, 1024 * w + 128 * hp:1024 * w + 128 * hp + 128]
                        wrot = WR[:, 1024 * w + 128 * hp:1024 * w + 128 * hp + 128]
                        g, f = G.take()
                        p = pe(mm(g.buf[:, :], wcol, src), t_wq, x_ready[b], *f)
                        a = act(i_activation(SQ[:, 2 * i + w, :], g.buf[:, :], ACT.Square),
                                p, st.get("sq"))
                        sqt.append(a)
                        t1, f = Tr.take()
                        d1 = dve(i_tensor_tensor(t1.buf[:, :], g.buf[:, :], TAB[:, 2 * w, :], ALU.mult),
                                 a, t_tab, *f)
                        g.free = [d1]
                        g, f = G.take()
                        p = pe(mm(g.buf[:, :], wrot, src), t_wr, *f)
                        t2, f = Tr.take()
                        d2 = dve(i_tensor_tensor(t2.buf[:, :], g.buf[:, :], TAB[:, 2 * w + 1, :], ALU.mult),
                                 p, *f)
                        g.free = [d2]
                        dst = Q[:, hp, :] if w == 0 else K[:, hp, 32:32 + L]
                        r = pool(i_tensor_tensor(dst, t1.buf[:, :], t2.buf[:, :], ALU.add),
                                 d1, d2, st["k"][hp])
                        t1.free = [r]
                        t2.free = [r]
                        raw.append(r)
                        yield
                wq_reads.append(p)
                g, f = G.take()
                for i in range(8):
                    for k in range(4):
                        p = pe(mm(g.buf[:, 16 * k + 2 * i:16 * k + 2 * i + 2], SQ[:, i, 128 * k:128 * k + 128], cn("hsel")),
                               sqt, *f)
                st["sq"] = p
                d = dve(i_tensor_scalar(ssb[:, :], g.buf[:, 0:64], 1e-24, None, ALU.max), p, st.get("rsb"))
                g.free = [d]
                yield
                r = power(rsb[:, :], ssb[:, :], 64, d, st.get("rsb"))
                g, f = G.take()
                for k in range(4):
                    p = pe(i_transpose(g.buf[0:16, 128 * k:128 * k + 128], rsb[:, 16 * k:16 * k + 16], ident),
                           r, *f)
                st["rsb"] = p
                yield
                d1 = dve(i_tensor_copy(R[0:16, :], g.buf[0:16, :]), p, st.get("R"), c5)
                d2 = dve(i_tensor_tensor(R[32:48, :], g.buf[0:16, :], R[0:16, :].bitcast(F32), ALU.subtract), d1)
                g.free = [d2]
                yield
                for i in range(4):
                    hp = 4 * hf + i
                    fin = []
                    for w in range(2):
                        g, f = G.take()
                        n = 2 * i + w
                        p = pe(mm(g.buf[:, :], bselr[:, 128 * n:128 * n + 128], R[:, :]), d1, d2, c2, *f)
                        dst = Q[:, hp, :] if w == 0 else K[:, hp, 32:32 + L]
                        d = dve(i_tensor_tensor(dst, dst, g.buf[:, :], ALU.mult), p, raw[2 * i + w])
                        g.free = [d]
                        fin.append(d)
                    qk_ready[(b, hp)] = fin
                    yield
                st["R"] = p

            def attend(b, hp):
                heads = []
                mt, f = Mr.take()
                for s in range(2):
                    sk, f2 = S.take()
                    p = pe(mm(sk.buf[:, :], identb[:, :], maskb[:, :], True, False, skip_group_check=True), c3, c4, *f2)
                    for t, (q0, nq) in enumerate(QB):
                        m = 128 if t < 5 else 64
                        p = pe(mm(sk.buf[0:m, q0:q0 + nq], K[64 * s:64 * s + 64, hp, 96 * t:96 * t + m],
                                  Q[64 * s:64 * s + 64, hp, q0:q0 + nq], False, False, skip_group_check=True),
                               qk_ready[(b, hp)], z1)
                    d = dve(i_tensor_reduce(
                        mt.buf[:, 16 * s:16 * s + 16], sk.buf[:, :].rearrange("p (a c) -> p a c", c=32), AX_X, ALU.max,
                        apply_transpose=True), p, *f)
                    heads.append((sk, d))
                st["k"][hp] = p
                yield
                g, f = G.take()
                p = pe(i_transpose(g.buf[0:32, 0:128], mt.buf[:, 0:32], ident), heads[0][1], heads[1][1], *f)
                d = dve(i_tensor_reduce(
                    mt.buf[0:32, 32:64], g.buf[0:32, 0:128].rearrange("p (k c) -> p c k", k=4), AX_X, ALU.max), p)
                g.free = [d]
                er, f = Er.take()
                ep = pool(i_tensor_tensor(
                    er.buf[:, :].rearrange("p (a c) -> p a c", a=16),
                    mt.buf[0:32, 32:64].rearrange("p (o c) -> p o c", o=1).broadcast_to([32, 16, 32]),
                    cn("mske", 32).rearrange("p (a o) -> p a o", o=1).broadcast_to([32, 16, 32]), ALU.mult), d, *f)
                mt.free = [ep]
                yield
                pts = []
                for s in range(2):
                    sk = heads[s][0]
                    p = pe(mm(sk.buf[:, :], nselr[:, 128 * s:128 * s + 128], er.buf[:, :], False, True, skip_group_check=True),
                           ep, c1)
                    pt, f = Pr.take()
                    a = act(i_activation(pt.buf[:, :], sk.buf[:, :], ACT.Exp), p, *f)
                    sk.free = [a]
                    pts.append((pt, a))
                er.free = [p]
                yield
                f_y, f_s = yb.free, sb_bank.free
                for s in range(2):
                    p1 = pe(mm(sb_bank.buf[64 * s:64 * s + 64, :], cn("ones")[:, 0:64], pts[s][0].buf[:, :]), pts[s][1], f_s)
                for t, (q0, nq) in enumerate(QB):
                    m = 128 if t < 5 else 64
                    for s in range(2):
                        h = 2 * hp + s
                        p = pe(mm(yb.buf[64 * s:64 * s + 64, q0:q0 + nq], V[0:m, t, 64 * h:64 * h + 64],
                                  pts[s][0].buf[0:m, q0:q0 + nq]), v_ready[b], f_y)
                for s in range(2):
                    pts[s][0].free = [p]
                st["v_next"] = p
                rc, f = Tr.take()
                d = dve(i_reciprocal(rc.buf[:, :], sb_bank.buf[:, :]), p1, *f)
                sb_bank.free = [d]
                d2 = dve(i_tensor_tensor(AO[:, hp, :], yb.buf[:, :], rc.buf[:, :], ALU.mult), d, p,
                         st["ao"])
                yb.free = [d2]
                rc.free = [d2]
                st["ao_w"] = d2
                yield

            def outproj(b):
                g, f = G.take()
                for i in range(8):
                    p = pe(mm(g.buf[:, :], WO[:, i, :], AO[:, i, :], i == 0, i == 7), st["ao_w"], t_wo, *f)
                st["ao"] = p
                x0, x1 = X[0:64, b, 32:32 + L], X[64:128, b, 33:33 + L]
                d1 = dve(i_tensor_tensor(x0, g.buf[0:64, :], x0, ALU.add), p, x_ready[b])
                d2 = dve(i_tensor_tensor(x1, g.buf[64:128, :], x1, ALU.add), p, x_ready[b])
                g.free = [d1, d2]
                x_ready[b] = [d1, d2]
                wo_done[:] = [p]
                yield

            def attend_half(b, hf):
                before = None
                for i in range(4):
                    g = attend(b, 4 * hf + i)
                    steps(g, 1)
                    yield
                    if before:
                        steps(before, 9)
                        yield
                    steps(g, 1)
                    yield
                    steps(g, 1)
                    before = g
                    yield
                steps(before, 9)
                yield

            def side(b, hf):
                yield from attend_half(b, hf)
                if hf == 1:
                    st["v"] = st["v_next"]
                    yield from outproj(b)

            halves = [(b, hf) for b in range(NB) for hf in range(2)]
            run(proj(0, 0), vproj(0))
            for n, (b, hf) in enumerate(halves):
                nxt = halves[n + 1] if n + 1 < len(halves) else None
                gens = [side(b, hf)]
                if nxt:
                    gens.append(proj(*nxt))
                run(*gens)
                if nxt and nxt[1] == 0:
                    run(vproj(nxt[0]))
            wq_done = wq_reads[-2:]
            tab_done = [g for g in [x_ready[NB - 1]] for g in g]

            q.phase += 1

            def ffn(b):
                src = X[:, b, 32:32 + L]
                xc, d, rr, d3 = yield from norm([(cmt, src)], [x_ready[b]])
                yield
                m = dve(i_tensor_tensor(xc.buf[:, :], xc.buf[:, :], rr.buf[:, :], ALU.mult), d, d3)
                m2 = dve(i_tensor_scalar(rr.buf[:, :], xc.buf[:, :], VEC[:, layer, 0:1], VEC[:, layer, 1:2],
                                                   ALU.mult, ALU.add), m, t_v)
                xc.free = [m2]
                yield
                hs = []
                for i, (o, n) in enumerate(FP):
                    ga, f = G.take()
                    pa = pe(mm(ga.buf[0:n, :], W1[:, o:o + n], rr.buf[:, :]), m2, t_w1, *f)
                    gg, f = G.take()
                    pg = pe(mm(gg.buf[0:n, :], W1[:, F1 + o:F1 + o + n], rr.buf[:, :]), *f)
                    h, f = Tr.take()
                    a = act(i_activation(h.buf[0:n, :], gg.buf[0:n, :], ACT.Gelu,
                                                                        bias=VEC[0:n, layer, 5 + i:6 + i]), pg, *f)
                    gg.free = [a]
                    d = dve(i_scalar_tensor_tensor(
                        h.buf[0:n, :], ga.buf[0:n, :], VEC[0:n, layer, 2 + i:3 + i], h.buf[0:n, :], ALU.add, ALU.mult), pa, a)
                    ga.free = [d]
                    hs.append((h, d))
                    yield
                rr.free = [pg]
                g, f = S.take()
                for i, (o, n) in enumerate(FP):
                    p = pe(mm(g.buf[:, :], W2[0:n, i, :], hs[i][0].buf[0:n, :], i == 0, i == 2), hs[i][1], t_w2, *f)
                for h, _ in hs:
                    h.free = [p]
                x0, x1 = X[0:64, b, 32:32 + L], X[64:128, b, 33:33 + L]
                d1 = dve(i_scalar_tensor_tensor(x0, g.buf[0:64, :], VEC[0:64, layer, 8:9], x0, ALU.add, ALU.add), p, x_ready[b])
                d2 = dve(i_scalar_tensor_tensor(x1, g.buf[64:128, :], VEC[64:128, layer, 8:9], x1, ALU.add, ALU.add), p, x_ready[b])
                g.free = [d1, d2]
                x_ready[b] = [d1, d2]
                w12_done[:] = [p]
                yield

            gens = [ffn(b) for b in range(NB)]
            live = [gens.pop(0)]
            n = 0
            while live:
                for g in list(live):
                    if not steps(g):
                        live.remove(g)
                n += 1
                if gens and len(live) < 2 and n >= 4:
                    live.append(gens.pop(0))
            w12_done = list(w12_done)

        q.phase += 1
        outs = []

        def final(b):
            u, f = Tr.take()
            a1 = act(i_copy(u.buf[0:64, :], X[0:64, b, 32:32 + L]), x_ready[b], *f)
            a2 = act(i_copy(u.buf[64:128, :], X[64:128, b, 33:33 + L]), x_ready[b])
            r, f = Tr.take()
            t_r = dma(r.buf[:, :], x1d[:, b, :], f"x{b % 2}", x1_store[b], *f)
            yield
            xc, d, rr, d3 = yield from norm([(cmt, u.buf[:, :])], [a1, a2])
            yield
            m = dve(i_tensor_tensor(xc.buf[:, :], xc.buf[:, :], rr.buf[:, :], ALU.mult), d, d3)
            m = pool(i_tensor_tensor(r.buf[:, :], r.buf[:, :], xc.buf[:, :], ALU.add), m, t_r)
            xc.free = [m]
            rr.free = [m]
            g, f = G.take()
            for i in range(4):
                p = pe(i_transpose(g.buf[:, 128 * i:128 * i + 128], r.buf[:, 128 * i:128 * i + 128], ident),
                       m, *f)
            a = act(i_copy(u.buf[:, :], g.buf[:, :]), p, d)
            g.free = [a]
            r.free = [p]
            t = dma(out[b].rearrange("(a p) d -> p a d", p=128), u.buf[:, :].rearrange("p (a d) -> p a d", a=4), f"o{b}", a)
            u.free = [t]
            outs.append(t)
            yield

        for b in range(0, NB, 2):
            run(final(b), final(b + 1))
        op("sp", None, outs, list(x1_store))

        q.number(lambda n: ctx.enter_context(nc.semaphore(n)))
        block = ctx.enter_context(nc.Block())

        @block.sync
        def _(e):
            q.emit("sp", e)

        @block.tensor
        def _(e):
            q.emit("pe", e)

        @block.vector
        def _(e):
            q.emit("dve", e)

        @block.scalar
        def _(e):
            q.emit("act", e)

        @block.gpsimd
        def _(e):
            q.emit("pool", e)


def kernel(**inputs):
    import numpy as _np
    import concourse.bacc as _bacc
    from concourse import mybir as _mybir
    from concourse.bass_utils import run_bass_kernel_spmd as _run

    g = {k: _np.asarray(v) for k, v in inputs.items()}
    vec = _np.zeros((128, DEPTH, 16), _np.float32)
    for l in range(DEPTH):
        vec[:, l, 0] = g["L0_ffn_ln_g"][l]
        vec[:, l, 1] = g["L0_ffn_ln_b"][l]
        for i, (o, n) in enumerate(FP):
            vec[0:n, l, 2 + i] = g["L0_ffn_b1"][l, o:o + n]
            vec[0:n, l, 5 + i] = g["L0_ffn_b1"][l, F1 + o:F1 + o + n]
        vec[:, l, 8] = g["L0_ffn_b2"][l]
        for i, n in enumerate(("L0_ffn_q_scale", "L0_ffn_k_scale")):
            s = g[n][l]
            for h in range(2):
                vec[64 * h:64 * h + 64, l, 9 + 2 * i] = s
                vec[64 * h:64 * h + 32, l, 10 + 2 * i] = s[32:64]
                vec[64 * h + 32:64 * h + 64, l, 10 + 2 * i] = s[0:32]
        for h in range(2):
            vec[64 * h:64 * h + 64, l, 13] = g["L0_attn_g_weight"]
    wo = _np.ascontiguousarray(g["L0_attn_Wo"].T.reshape(8, 128, 128).transpose(1, 0, 2).reshape(128, 1024))
    data = [
        ("x", g["L0_attn_hidden_states"]), ("cst", constants()),
        ("awq", g["L0_attn_Wq"].T), ("awk", g["L0_attn_Wk"].T), ("awv", g["L0_attn_Wv"].T), ("awo", wo),
        ("wqkv", g["L0_ffn_Wqkv"]), ("wo", g["L0_ffn_Wo"]), ("w1", g["L0_ffn_W1"]), ("w2", g["L0_ffn_W2"]), ("vec", vec),
    ]
    nc = _bacc.Bacc("TRN2", target_bir_lowering=False, num_devices=1)
    arrays, args = {}, []
    for name, a in data:
        a = _np.ascontiguousarray(a)
        arrays["in_" + name] = a
        args.append(nc.dram_tensor("in_" + name, a.shape, _mybir.dt.from_np(a.dtype), kind="ExternalInput").ap())
    o = nc.dram_tensor("out_0", (NB, L, D), F32, kind="ExternalOutput").ap()
    build(nc, *args, o)
    r = _run(nc, [arrays], core_ids=[0])
    return r.results[0]["out_0"]
```

```python
from contextlib import ExitStack

import numpy as np
import concourse.bass as bass
from concourse import mybir

F32 = mybir.dt.float32
F32R = mybir.dt.float32r
BF16 = mybir.dt.bfloat16
ACT = mybir.ActivationFunctionType
ALU = mybir.AluOpType
AX_X = mybir.AxisListType.X

NB, L, D = 8, 512, 128
DEPTH = 6
F1 = 341
FP = [(0, 114), (114, 114), (228, 113)]
EPS = 1e-5
NEG = -1.0e30
QB = [(96 * t, min(96, L - 96 * t)) for t in range(6)]

CONST = {}
CONST_COLS = 0
for _n, _w in (("ident", 128), ("cm", 128), ("om", 1), ("one", 1), ("tri", 128), ("hsel", 2), ("cum", 12), ("mske", 16),
               ("hilo", 2), ("tab", 2048), ("nsel", 256), ("bsel", 1024), ("mask", 512)):
    CONST[_n] = (CONST_COLS, _w)
    CONST_COLS += _w
KEPT = CONST["nsel"][0]


def constants():
    c = np.zeros((128, CONST_COLS), np.float32)

    def part(n):
        o, w = CONST[n]
        return c[:, o:o + w]

    eye = np.eye(128, dtype=np.float32)
    part("ident")[:] = eye
    part("cm")[:] = eye - np.float32(1.0 / 128)
    part("om")[:] = 1.0 / 128
    r = np.arange(128)
    part("one")[:] = 1.0
    part("tri")[:] = r[:, None] <= r[None, :]
    part("hsel")[:] = r[:, None] // 64 == np.arange(2)[None, :]
    for j in range(3):
        for i in range(4):
            part("cum")[:, 4 * j + i] = float(i > j)
    for p in range(32):
        part("mske")[p, p % 16] = 1.0
        part("nsel")[p, 128 * (p // 16):128 * (p // 16) + 128] = -1.0
    part("hilo")[:, 0] = -1.0 * (r % 64 // 16 == 1)
    part("hilo")[:, 1] = -1.0 * (r % 64 // 16 == 2)
    for i in range(8):
        for s in range(2):
            for base in (0, 32):
                part("bsel")[base + 2 * i + s, 128 * i + 64 * s:128 * i + 64 * s + 64] = 1.0
    half = np.arange(0, 64, 2, dtype=np.float32)
    inv_freq = (1.0 / np.float32(10000.0) ** (half / np.float32(64))).astype(np.float32)
    t = np.arange(L, dtype=np.float32)
    freqs = (t[:, None] * inv_freq[None, :]).astype(np.float32)
    base = ((half + 0.4 * 64) / (1.4 * 64)).astype(np.float64)
    power = (np.arange(L) - L // 2) / 16.0
    scale = base[None, :] ** power[:, None]
    cos, sin = np.cos(freqs.astype(np.float64)), np.sin(freqs.astype(np.float64))
    sgn = np.where(np.arange(64) < 32, -1.0, 1.0)

    def dims(a):
        return np.concatenate([a, a], 1)

    tabs = [dims(cos * scale) * 8.0, dims(sin * scale) * sgn * 8.0, dims(cos / scale), dims(sin / scale) * sgn]
    for i, a in enumerate(tabs):
        part("tab")[:, 512 * i:512 * i + 512] = np.concatenate([a.T, a.T], 0)
    m = np.full((128, L), NEG, np.float32)
    for ti, (q0, nq) in enumerate(QB):
        for q in range(q0, q0 + nq):
            for rr in range(128):
                j = q0 - 32 + rr
                if 0 <= j < L and 0 <= q - j <= 32:
                    m[rr, q] = 0.0
    part("mask")[:] = m
    return c


class Tok:

    def __init__(self, eng):
        self.eng, self.used, self.sem, self.val = eng, False, None, 0


class Queues:

    def __init__(self):
        self.q = {e: [] for e in ("pe", "act", "dve", "pool", "sp")}
        self.phase = 0

    def op(self, eng, fn, *after, sem=None):
        tok = Tok(eng)
        flat = []
        for a in after:
            flat += a if isinstance(a, list) else [a]
        flat = [a for a in flat if a is not None]
        for a in flat:
            a.used = True
        self.q[eng].append((fn, flat, tok, sem, self.phase))
        return tok

    def number(self, new_sem):
        sems, counts = {}, {}
        for eng, ops in self.q.items():
            for fn, after, tok, sem, phase in ops:
                if sem is None and not tok.used:
                    continue
                key = sem if sem is not None else (eng, phase)
                if key not in sems:
                    sems[key] = new_sem("s_" + "_".join(str(x) for x in (key if isinstance(key, tuple) else (key,))))
                    counts[key] = 0
                counts[key] += 16 if sem is not None else 1
                tok.sem, tok.val = sems[key], counts[key]
                tok.key = key

    def emit(self, eng, e):
        seen = {}
        for fn, after, tok, sem, phase in self.q[eng]:
            for a in after:
                if seen.get(a.key, 0) < a.val:
                    e.wait_ge(a.sem, a.val)
                    seen[a.key] = a.val
            if fn is None:
                continue
            ins = fn(e)
            if tok.sem is not None:
                ins.then_inc(tok.sem, 16 if sem is not None else 1)


class Slot:

    def __init__(self, buf, ring=None):
        self.buf, self.ring, self.after = buf, ring, []

    @property
    def free(self):
        return self.after

    @free.setter
    def free(self, toks):
        self.after = toks
        if self.ring is not None:
            assert self not in self.ring, "given back twice"
            self.ring.append(self)


class Ring:

    def __init__(self, bufs):
        self.idle = []
        self.idle += [Slot(b, self.idle) for b in bufs]

    def take(self):
        assert self.idle, "every buffer is in use"
        s = self.idle.pop(0)
        return s, s.after


def i_activation(*a, **k):
    return lambda e: e.activation(*a, **k)


def i_copy(*a, **k):
    return lambda e: e.copy(*a, **k)


def i_memset(*a, **k):
    return lambda e: e.memset(*a, **k)


def i_reciprocal(*a, **k):
    return lambda e: e.reciprocal(*a, **k)


def i_scalar_tensor_tensor(*a, **k):
    return lambda e: e.scalar_tensor_tensor(*a, **k)


def i_tensor_copy(*a, **k):
    return lambda e: e.tensor_copy(*a, **k)


def i_tensor_reduce(*a, **k):
    return lambda e: e.tensor_reduce(*a, **k)


def i_tensor_scalar(*a, **k):
    return lambda e: e.tensor_scalar(*a, **k)


def i_tensor_tensor(*a, **k):
    return lambda e: e.tensor_tensor(*a, **k)


def i_transpose(*a, **k):
    return lambda e: e.transpose(*a, **k)


def mm(o, lhsT, rhs, start=True, stop=True, **kw):
    return lambda e: e.matmul(o, lhsT, rhs, start=start, stop=stop, **kw)


def run(*gens):
    gens = list(gens)
    while gens:
        for g in list(gens):
            if not steps(g):
                gens.remove(g)


def until(g):
    for mark in g:
        if mark:
            return
        yield


def steps(g, n=1):
    for _ in range(n):
        try:
            next(g)
        except StopIteration:
            return False
    return True


def build(nc, xin, cst, awq, awk, awv, awo, wqkv, wo, w1, w2, vec, out):
    with ExitStack() as ctx:
        def sb(name, shape, dt=F32, c=ctx):
            return c.enter_context(nc.sbuf_tensor(name, shape, dt))

        x1d = nc.dram_tensor("x1_scratch", (128, NB, L), F32, kind="Internal").ap()
        bank = [ctx.enter_context(nc.psum_tensor(f"bank{i}", [128, 512], F32)) for i in range(8)]
        X = sb("X", [128, NB, L + 33])
        C = sb("C", [128, KEPT])
        WH = sb("WH", [128, 5120], F32R)
        WL = sb("WL", [128, 5120], F32R)
        WO = sb("WO", [128, 8, 128])
        W1H = sb("W1H", [128, 2 * F1], F32R)
        W1L = sb("W1L", [128, 2 * F1], F32R)
        W2 = sb("W2", [128, 3, 128])
        VEC = sb("VEC", [128, DEPTH, 16])
        V = sb("V", [128, 6, 1024])
        AO = sb("AO", [128, 8, L])
        nselr = sb("nselr", [32, 256], F32R)
        bselr = sb("bselr", [64, 1024], F32R)
        identb = sb("identb", [128, 128], BF16)
        maskb = sb("maskb", [128, L], BF16)
        cumt = sb("cumt", [128, 32])
        VAR = sb("VAR", [128, 4, 64])
        Tr = Ring([sb(f"T{i}", [128, L]) for i in range(7)])
        Qr = Ring([sb(f"sq{i}", [128, L]) for i in range(3)])
        Rr = Ring([sb(f"R{i}", [64, L], F32R) for i in range(2)])
        Xr = Ring([(sb(f"XH{i}", [128, L + 33], F32R), sb(f"XL{i}", [128, L + 33], F32R)) for i in range(2)])
        Er = Ring([sb(f"E{i}", [32, L], F32R) for i in range(2)])
        Pr = Ring([sb(f"P{i}", [128, L]) for i in range(4)])
        Mr = Ring([sb(f"M{i}", [128, 64]) for i in range(3)])
        Nr = Ring([sb(f"N{i}", [128, 4, 64]) for i in range(3)])
        with ExitStack() as ca:
            QA = sb("QA", [128, 8, L], F32R, ca)
            KA = sb("KA", [128, 8, L], F32R, ca)
        Q = sb("Q", [128, 8, L])
        K = sb("K", [128, 8, L + 32])
        G = Ring(bank[0:3])
        S = Ring(bank[3:6])
        yb, ssb = Slot(bank[6]), Slot(bank[7])
        Vf = V[:, :, :].rearrange("p a b -> p (a b)")

        def cn(n, rows=128):
            o, w = CONST[n]
            return C[0:rows, o:o + w]

        q = Queues()
        op = q.op

        def pe(fn, *a):
            return op("pe", fn, *a)

        def act(fn, *a):
            return op("act", fn, *a)

        def dve(fn, *a):
            return op("dve", fn, *a)

        def pool(fn, *a):
            return op("pool", fn, *a)

        def dma(o, i, key, *a):
            return op("sp", lambda e: e.dma_start(o, i), *a, sem=key)

        def split(eng, hi, lo, src, *a):
            t1 = act(i_copy(hi, src), *a)
            t2 = eng(i_tensor_tensor(lo, src, hi.bitcast(F32), ALU.subtract), t1)
            return [t1, t2]

        def mm3(o, lh, ll, rh, rl, *a):
            pe(mm(o, lh, rh, True, False), *a)
            pe(mm(o, lh, rl, False, False), *a)
            return pe(mm(o, ll, rh, False, True), *a)

        t_c = dma(C[:, :], cst[:, 0:KEPT], "c")
        t_v = dma(VEC[:, :, :], vec, "v")
        n_sel = CONST_COLS - KEPT
        t_s = dma(Vf[:, 0:n_sel], cst[:, KEPT:CONST_COLS], "c2")
        t_aq = dma(Vf[:, 2048:2304], awq, "w0")
        t_ak = dma(Vf[:, 2304:2560], awk, "w1")
        t_av = dma(Vf[:, 2560:3584], awv, "w2")
        t_ao = dma(WO[:, :, :], awo.rearrange("p (c d) -> p c d", c=8), "w3")
        z0 = pool(i_memset(X[:, :, 0:33], 0.0))
        z2 = pool(i_memset(Vf[:, 3584:5632], 0.0))
        c5 = pool(i_memset(Rr.idle[0].buf[:, :].bitcast(F32), 0.0))
        c6 = pool(i_memset(Rr.idle[1].buf[:, :].bitcast(F32), 0.0))
        c1 = dve(i_tensor_copy(nselr[:, :], Vf[0:32, 0:256]), t_s)
        c2 = dve(i_tensor_copy(bselr[:, :], Vf[0:64, 256:1280]), t_s)
        c4 = dve(i_tensor_copy(maskb[:, :], Vf[:, 1280:1792]), t_s)
        c3 = dve(i_tensor_copy(identb[:, :], cn("ident")), t_c)
        t_wa = []
        for n, tw in ((0, t_aq), (1, t_ak)):
            dst = Vf[:, 3584 + 1024 * n:4608 + 1024 * n].rearrange("p (h c) -> p h c", c=64)
            src = Vf[:, 2048 + 256 * n:2304 + 256 * n].rearrange("p (h c) -> p h c", c=16)
            cp = [pool(i_tensor_copy(dst[:, :, 16 * i:16 * i + 16], src), tw, z2) for i in range(3)]
            for i in range(2):
                a, b = 1024 * n + 512 * i, 3584 + 1024 * n + 512 * i
                t_wa += split(dve, WH[:, a:a + 512], WL[:, a:a + 512], Vf[:, b:b + 512], cp)
        for i in range(2):
            t_wa += split(dve, WH[:, 2048 + 512 * i:2560 + 512 * i], WL[:, 2048 + 512 * i:2560 + 512 * i],
                          Vf[:, 2560 + 512 * i:3072 + 512 * i], t_av)
        stage_read = [c1, c2, c4] + t_wa
        ident = cn("ident")
        cmt = cn("cm")

        def rsqrt(nt, n, *a):
            v, r, u, w = (nt[:, i, 0:n] for i in range(4))
            t = act(i_activation(u, v, ACT.Ln), *a)
            t = act(i_activation(r, u, ACT.Exp, scale=-0.5), t)
            t = dve(i_tensor_tensor(u, v, r, ALU.mult), t)
            t = dve(i_scalar_tensor_tensor(u, u, -0.5, r, ALU.mult, ALU.mult), t)
            return dve(i_scalar_tensor_tensor(w, u, 1.5, r, ALU.add, ALU.mult), t)

        def spread(src, *a):
            g, f = G.take()
            for k in range(4):
                p = pe(mm(g.buf[:, 128 * k:128 * k + 128], src[:, k:k + 1].broadcast_to([128, 128]), ident), *a, f)
            return g, p

        def variance(dst, src, *a, keep=None):
            g, f = G.take()
            p = pe(mm(g.buf[:, :], cmt, src), *a, f, t_c)
            sq, f = Qr.take()
            t_sq = act(i_activation(sq.buf[:, :], g.buf[:, :], ACT.Square), p, f)
            g.free = [t_sq]
            if keep is not None:
                g.after += keep_copy(keep, g)
            yield
            g2, f = G.take()
            for k in range(4):
                p = pe(mm(g2.buf[:, k:k + 1], sq.buf[:, 128 * k:128 * k + 128], cn("om")), t_sq, f)
            sq.free = [p]
            t = dve(i_tensor_scalar(dst, g2.buf[:, 0:4], EPS, None, ALU.add), p, *a)
            g2.free = [t]
            yield
            return t

        def keep_copy(keep, g):
            keep["t"] = act(i_copy(keep["xc"].buf[:, :], g.buf[:, :]), keep["f"])
            return [keep["t"]]

        def norm(src, *a):
            nt, f1 = Nr.take()
            xc, f2 = Tr.take()
            keep = {"xc": xc, "f": f2}
            t = yield from variance(nt.buf[:, 0, 0:4], src, *a, f1, keep=keep)
            t = rsqrt(nt.buf, 4, t)
            yield
            gr, p = spread(nt.buf[:, 3, 0:4], t)
            nt.free = [p]
            return xc, gr, [keep["t"], p]

        def rows(src, cols, *a):
            g, f = G.take()
            for k in range(4):
                p = pe(i_transpose(g.buf[0:cols, 128 * k:128 * k + 128], src[:, cols * k:cols * k + cols], ident), *a, f)
            r, f = Rr.take()
            t1 = dve(i_tensor_copy(r.buf[0:cols, :], g.buf[0:cols, :]), p, f, c5, c6)
            t2 = dve(i_tensor_tensor(r.buf[32:32 + cols, :], g.buf[0:cols, :], r.buf[0:cols, :].bitcast(F32), ALU.subtract), t1)
            g.free = [t2]
            return r, p, [t1, t2]

        def pair_rows(r, i, *a):
            g, f = G.take()
            return g, pe(mm(g.buf[:, :], bselr[:, 128 * i:128 * i + 128], r.buf[:, :]), c2, *a, f)

        x_ready = [None] * NB
        x1_store = [None] * NB
        xa_of, xs_of, v_of = {}, {}, {}
        sa = {"v": stage_read, "ao": None, "cum": None, "k": [None] * 8}
        qa_ready = {}

        def a_load(b):
            s0, f = Tr.take()
            t_x = dma(s0.buf[:, :].rearrange("p (a d) -> p a d", a=4), xin[b].rearrange("(a p) d -> p a d", p=128),
                      f"x{b % 2}", f)
            g, f = G.take()
            for i in range(4):
                p = pe(i_transpose(g.buf[:, 128 * i:128 * i + 128], s0.buf[:, 128 * i:128 * i + 128], ident), t_x, t_c, f)
            xa, f = Tr.take()
            s0.free = [p]
            t_xa = act(i_copy(xa.buf[:, :], g.buf[:, :]), p, f)
            g.free = [t_xa]
            xa_of[b] = (xa, t_xa)
            yield
            xc, gr, t = yield from norm(xa.buf[:, :], t_xa)
            t_xn = dve(i_tensor_tensor(xc.buf[:, :], xc.buf[:, :], gr.buf[:, :], ALU.mult), t)
            gr.free = [t_xn]
            xs, f = Xr.take()
            t = split(pool, xs.buf[0][:, 0:L], xs.buf[1][:, 0:L], xc.buf[:, :], t_xn, f)
            xc.free = t
            xs_of[b] = (xs, t)
            yield

        def a_qk(b, hf):
            xs, t_xs = xs_of[b]
            xh, xl = (z[:, 0:L] for z in xs.buf)
            for hp in range(4 * hf, 4 * hf + 4):
                toks = []
                for n, dst in ((0, QA), (1, KA)):
                    c = slice(1024 * n + 128 * hp, 1024 * n + 128 * hp + 128)
                    g, f = G.take()
                    p = mm3(g.buf[:, :], WH[:, c], WL[:, c], xh, xl, t_xs, t_wa, f)
                    h, f = Tr.take()
                    t = act(i_copy(h.buf[:, :].bitcast(F32R), g.buf[:, :]), p, f)
                    t = dve(i_scalar_tensor_tensor(dst[:, hp, :], h.buf[:, :], cn("hilo")[:, n:n + 1], g.buf[:, :],
                                                   ALU.mult, ALU.add), t, sa["k"][hp])
                    g.free = [t]
                    h.free = [t]
                    toks.append(t)
                    yield
                qa_ready[(b, hp)] = toks

        def a_v(b):
            xs, t_xs = xs_of[b]
            xh, xl = xs.buf
            toks = []
            for i in range(4):
                for n in range(2):
                    c = slice(2048 + 512 * n, 2560 + 512 * n)
                    k = slice(128 * i, 128 * i + 128)
                    g, f = G.take()
                    p = mm3(g.buf[:, :], xh[:, k], xl[:, k], WH[:, c], WL[:, c], t_xs, t_wa, f)
                    t = act(i_copy(V[:, i, 512 * n:512 * n + 512], g.buf[:, :]), p, sa["v"])
                    g.free = [t]
                    toks.append(t)
                yield
            xs.free = [p]
            g, f = G.take()
            for h in range(8):
                for j in range(3):
                    p = pe(mm(g.buf[:, 4 * h:4 * h + 4], V[:, j, 128 * h:128 * h + 128], cn("cum")[:, 4 * j:4 * j + 4],
                              h == 0 and j == 0, h == 7 and j == 2, skip_group_check=True), toks, f)
            t = dve(i_tensor_copy(cumt[:, :], g.buf[:, 0:32]), p, sa["cum"])
            g.free = [t]
            v_of[b] = (toks, t)
            yield

        def a_attend(b):
            t_v_ready, t_cum = v_of[b]
            t_y, ss = [], []
            f_ss = ssb.free
            for hp in range(8):
                f_y = yb.free
                for j in range(4):
                    pts = []
                    n = L - 128 * j
                    for s in range(2):
                        st, f = S.take()
                        r0 = 64 * s
                        p = pe(mm(st.buf[:, 0:n], KA[r0:r0 + 64, hp, 128 * j:128 * j + 128], QA[r0:r0 + 64, hp, 128 * j:512]),
                               qa_ready[(b, hp)], f)
                        pt, f = Pr.take()
                        t = act(i_activation(pt.buf[:, 0:n], st.buf[:, 0:n], ACT.Square, bias=1.0, scale=0.25), p, f)
                        st.free = [t]
                        t2 = dve(i_scalar_tensor_tensor(pt.buf[:, 0:128], pt.buf[:, 0:128], 1.0, cn("tri"),
                                                        ALU.add, ALU.mult), t)
                        pts.append((pt, [t, t2]))
                    if j == 3:
                        sa["k"][hp] = p
                    yield
                    for s in range(2):
                        h = 2 * hp + s
                        pt, tt = pts[s]
                        p2 = pe(mm(yb.buf[64 * s:64 * s + 64, 128 * j:512], V[:, j, 64 * h:64 * h + 64], pt.buf[:, 0:n],
                                   j == 0, j == 3), tt, t_v_ready, f_y)
                    for s in range(2):
                        pts[s][0].free = [p2]
                cb = cumt[:, 4 * hp:4 * hp + 4].rearrange("p (a o) -> p a o", o=1).broadcast_to([128, 4, 128])
                d = dve(i_tensor_tensor(AO[:, hp, :].rearrange("p (a c) -> p a c", a=4),
                                        yb.buf[:, :].rearrange("p (a c) -> p a c", a=4), cb, ALU.add), p2, t_cum, sa["ao"])
                yb.free = [d]
                sq, f = Qr.take()
                a = act(i_activation(sq.buf[:, :], AO[:, hp, :], ACT.Square), d, f)
                ss.append((sq, a))
                t_y.append(d)
                yield
                for sq, a in ss:
                    for k in range(4):
                        c = 16 * k + 2 * hp
                        p = pe(mm(ssb.buf[:, c:c + 2], sq.buf[:, 128 * k:128 * k + 128], cn("hsel")), a, f_ss)
                    sq.free = [p]
                ss = []
                if hp == 3:
                    yield True
            sa["v"] = p2
            sa["cum"] = t_y[-1]
            nt, f = Nr.take()
            t = dve(i_tensor_scalar(nt.buf[:, 0, :], ssb.buf[:, 0:64], 1.0 / 64, 4 * EPS, ALU.mult, ALU.add), p, f)
            ssb.free = [t]
            t = rsqrt(nt.buf, 64, t)
            yield
            r, p, t = rows(nt.buf[:, 3, :], 16, t)
            nt.free = [p]
            yield
            for hp in range(8):
                g, p = pair_rows(r, hp, t)
                t2 = dve(i_scalar_tensor_tensor(AO[:, hp, :], AO[:, hp, :], VEC[:, 0, 13:14], g.buf[:, :], ALU.mult, ALU.mult),
                         p, t_v, t_y[hp])
                g.free = [t2]
                t_y[hp] = t2
                if hp % 2:
                    yield
            r.free = [p]
            sa["y"] = t_y

        def a_out(b):
            xa, t_xa = xa_of.pop(b)
            g, f = G.take()
            for i in range(8):
                p = pe(mm(g.buf[:, :], WO[:, i, :], AO[:, i, :], i == 0, i == 7), sa["y"][i], t_ao, f)
            sa["ao"] = sa["wo"] = p
            z, f = Tr.take()
            t_z = act(i_copy(z.buf[:, :], g.buf[:, :]), p, f)
            g.free = [t_z]
            yield
            xc, gr, t = yield from norm(z.buf[:, :], t_z)
            m = dve(i_tensor_tensor(z.buf[:, :], xc.buf[:, :], gr.buf[:, :], ALU.mult), t)
            xc.free = [m]
            gr.free = [m]
            t_x1 = pool(i_tensor_tensor(xa.buf[:, :], xa.buf[:, :], z.buf[:, :], ALU.add), m, t_xa)
            x1_store[b] = dma(x1d[:, b, :], xa.buf[:, :], f"x1s{b}", t_x1)
            z.free = [t_x1]
            yield
            xc, gr, t = yield from norm(xa.buf[:, :], t_x1)
            xa.free = [x1_store[b], t[1]]
            m1 = dve(i_tensor_tensor(X[0:64, b, 32:32 + L], xc.buf[0:64, :], gr.buf[0:64, :], ALU.mult), t, z0)
            m2 = dve(i_tensor_tensor(X[64:128, b, 33:33 + L], xc.buf[64:128, :], gr.buf[64:128, :], ALU.mult), t, z0)
            xc.free = [m1, m2]
            gr.free = [m1, m2]
            x_ready[b] = [m1, m2]
            yield

        def a_next(b):
            yield from a_load(b)
            yield from a_qk(b, 0)

        run(a_next(0))
        run(a_v(0))
        for b in range(NB):
            att = a_attend(b)
            gens = []
            if b:
                gens = [a_out(b - 1)]
                steps(gens[0], 1)
            run(until(att), a_qk(b, 1), *gens)
            run(att, *([a_next(b + 1)] if b + 1 < NB else []))
            if b + 1 < NB:
                run(a_v(b + 1))
        run(a_out(NB - 1))
        end_a = sa["v"]
        wh_done = [v_of[NB - 1][1], sa["v"]]

        z1 = pool(i_memset(K[:, :, 0:32], 0.0), end_a)
        st = {"k": [end_a] * 8, "v": None, "ao": sa["wo"]}
        wo_done, w12_done = [sa["wo"]], []

        def load_split(layer, stage_free):
            t = dma(Vf[:, 0:3072], wqkv[layer], "w4", stage_free)
            t_w["1d"] = dma(Vf[:, 3072:3072 + 2 * F1], w1[layer], "w6", stage_free)
            toks = []
            for c in range(0, 3072, 512):
                toks += split(dve, WH[:, c:c + 512], WL[:, c:c + 512], Vf[:, c:c + 512], t, wh_done)
                yield
            for c in range(0, 2048, 512):
                src = Vf[:, c:c + 512].rearrange("p (h a c) -> p h a c", a=2, c=32)[:, :, ::-1, :]
                d = 3072 + c
                hi, lo = (w[:, d:d + 512].rearrange("p (h a c) -> p h a c", a=2, c=32) for w in (WH, WL))
                t1 = act(i_copy(hi, src), t, wh_done)
                toks += [t1, dve(i_tensor_tensor(lo, src, hi.bitcast(F32), ALU.subtract), t1)]
                yield
            t_w["qkv"] = toks

        def finish_w1(layer):
            t_w["1"] = split(dve, W1H[:, :], W1L[:, :], Vf[:, 3072:3072 + 2 * F1], t_w["1d"], w12_done)
            t_w["2"] = [dma(W2[0:n, i, :], w2[layer, o:o + n, :], f"w{7 + i}", w12_done) for i, (o, n) in enumerate(FP)]

        def load_wo(layer):
            t_w["o"] = dma(WO[:, :, :], wo[layer].rearrange("(c p) d -> p c d", p=128), "w5", wo_done)

        t_w = {}
        run(load_split(0, [sa["v"]]))
        finish_w1(0)
        load_wo(0)
        for layer in range(DEPTH):
            q.phase += 1
            v_ready, qk_ready, wq_reads = {}, {}, []
            t_wq = t_w["qkv"]
            st["v"] = t_w["1"] + t_wq
            tb = CONST["tab"][0]

            def xsplit(b):
                xs, f = Xr.take()
                t = split(pool, xs.buf[0][:, 0:L + 32], xs.buf[1][:, 0:L + 32], X[:, b, 0:L + 32], x_ready[b], f)
                xs_of[b] = (xs, t)

            def vproj(b):
                xs, t_xs = xs_of[b]
                xh, xl = xs.buf
                toks = []
                for t in range(6):
                    n = 128 if t < 5 else 64
                    k = slice(96 * t, 96 * t + n)
                    for c in range(2):
                        w = slice(2048 + 512 * c, 2560 + 512 * c)
                        g, f = G.take()
                        p = mm3(g.buf[0:n, :], xh[:, k], xl[:, k], WH[:, w], WL[:, w], t_wq, t_xs, f)
                        a = act(i_copy(V[0:n, t, 512 * c:512 * c + 512], g.buf[0:n, :]), p, st["v"])
                        g.free = [a]
                        toks.append(a)
                    yield
                v_ready[b] = toks
                wq_reads.append(p)

            def proj(b, hf):
                if hf == 0:
                    xsplit(b)
                xs, t_xs = xs_of[b]
                xh, xl = (z[:, 32:32 + L] for z in xs.buf)
                raw, wait = [], None
                f_ss = ssb.free
                for i in range(4):
                    hp = 4 * hf + i
                    for w in range(2):
                        c = slice(1024 * w + 128 * hp, 1024 * w + 128 * hp + 128)
                        cr = slice(3072 + c.start, 3072 + c.stop)
                        g, f = G.take()
                        p = mm3(g.buf[:, :], WH[:, c], WL[:, c], xh, xl, t_wq, t_xs, f)
                        sq, f = Qr.take()
                        a = act(i_activation(sq.buf[:, :], g.buf[:, :], ACT.Square), p, f)
                        t1, f = Tr.take()
                        d1 = dve(i_scalar_tensor_tensor(t1.buf[:, :], g.buf[:, :], VEC[:, layer, 9 + 2 * w:10 + 2 * w],
                                                        C[:, tb + 1024 * w:tb + 1024 * w + 512], ALU.mult, ALU.mult),
                                 a, t_c, t_v, f)
                        g.free = [d1]
                        g, f = G.take()
                        p = mm3(g.buf[:, :], WH[:, cr], WL[:, cr], xh, xl, f)
                        t2, f = Tr.take()
                        d2 = dve(i_scalar_tensor_tensor(t2.buf[:, :], g.buf[:, :], VEC[:, layer, 10 + 2 * w:11 + 2 * w],
                                                        C[:, tb + 512 + 1024 * w:tb + 1024 + 1024 * w], ALU.mult, ALU.mult),
                                 p, f)
                        g.free = [d2]
                        dst = Q[:, hp, :] if w == 0 else K[:, hp, 32:32 + L]
                        r = pool(i_tensor_tensor(dst, t1.buf[:, :], t2.buf[:, :], ALU.add), d1, d2, st["k"][hp])
                        t1.free = [r]
                        t2.free = [r]
                        raw.append(r)
                        if wait:
                            squares(*wait, f_ss)
                        wait = (sq, a, 2 * i + w)
                        yield
                wq_reads.append(p)
                if hf == 1:
                    xs.free = [p]
                p = squares(*wait, f_ss)
                nt, f = Nr.take()
                t = dve(i_tensor_scalar(nt.buf[:, 0, :], ssb.buf[:, 0:64], 1e-24, None, ALU.max), p, f)
                ssb.free = [t]
                t = rsqrt(nt.buf, 64, t)
                yield
                r, p, t = rows(nt.buf[:, 3, :], 16, t)
                nt.free = [p]
                yield
                for i in range(4):
                    hp = 4 * hf + i
                    fin = []
                    for w in range(2):
                        g, p = pair_rows(r, 2 * i + w, t)
                        dst = Q[:, hp, :] if w == 0 else K[:, hp, 32:32 + L]
                        d = dve(i_tensor_tensor(dst, dst, g.buf[:, :], ALU.mult), p, raw[2 * i + w])
                        g.free = [d]
                        fin.append(d)
                    qk_ready[(b, hp)] = fin
                    yield
                r.free = [p]

            def squares(sq, a, i, f_ss):
                for k in range(4):
                    c = 16 * k + 2 * i
                    p = pe(mm(ssb.buf[:, c:c + 2], sq.buf[:, 128 * k:128 * k + 128], cn("hsel")), a, f_ss)
                sq.free = [p]
                return p

            def attend(b, hp, sums):
                heads = []
                mt, f = Mr.take()
                sk = []
                for s in range(2):
                    k, f2 = S.take()
                    pe(mm(k.buf[:, :], identb[:, :], maskb[:, :], True, False, skip_group_check=True), c3, c4, f2)
                    sk.append(k)
                for t, (q0, nq) in enumerate(QB):
                    m = 128 if t < 5 else 64
                    for s in range(2):
                        p = pe(mm(sk[s].buf[0:m, q0:q0 + nq], K[64 * s:64 * s + 64, hp, 96 * t:96 * t + m],
                                  Q[64 * s:64 * s + 64, hp, q0:q0 + nq], False, False, skip_group_check=True),
                               qk_ready[(b, hp)], z1)
                d = [dve(i_tensor_reduce(mt.buf[:, 16 * s:16 * s + 16], sk[s].buf[:, :].rearrange("p (a c) -> p a c", c=32),
                                         AX_X, ALU.max, apply_transpose=True), p, f) for s in range(2)]
                st["k"][hp] = p
                yield
                g, f = G.take()
                p = pe(i_transpose(g.buf[0:32, 0:128], mt.buf[:, 0:32], ident), d, f)
                d = dve(i_tensor_reduce(mt.buf[0:32, 32:64], g.buf[0:32, 0:128].rearrange("p (k c) -> p c k", k=4),
                                        AX_X, ALU.max), p)
                g.free = [d]
                er, f = Er.take()
                ep = pool(i_tensor_tensor(
                    er.buf[:, :].rearrange("p (a c) -> p a c", a=16),
                    mt.buf[0:32, 32:64].rearrange("p (o c) -> p o c", o=1).broadcast_to([32, 16, 32]),
                    cn("mske", 32).rearrange("p (a o) -> p a o", o=1).broadcast_to([32, 16, 32]), ALU.mult), d, f)
                mt.free = [ep]
                yield
                pts = []
                for s in range(2):
                    p = pe(mm(sk[s].buf[:, :], nselr[:, 128 * s:128 * s + 128], er.buf[:, :], False, True,
                              skip_group_check=True), ep, c1)
                    pt, f = Pr.take()
                    a = act(i_activation(pt.buf[:, :], sk[s].buf[:, :], ACT.Exp), p, f)
                    sk[s].free = [a]
                    pts.append((pt, a))
                er.free = [p]
                yield
                f_y = yb.free
                for t, (q0, nq) in enumerate(QB):
                    m = 128 if t < 5 else 64
                    for s in range(2):
                        h = 2 * hp + s
                        p = pe(mm(yb.buf[64 * s:64 * s + 64, q0:q0 + nq], V[0:m, t, 64 * h:64 * h + 64],
                                  pts[s][0].buf[0:m, q0:q0 + nq]), pts[0][1], pts[1][1], v_ready[b], f_y)
                st["v_next"] = p
                t_y = act(i_copy(AO[:, hp, :], yb.buf[:, :]), p, st["ao"])
                yb.free = [t_y]
                g, f = G.take()
                for s in range(2):
                    for k in range(4):
                        c = 2 * k + s
                        p = pe(mm(g.buf[:, c:c + 1], pts[s][0].buf[:, 128 * k:128 * k + 128], cn("one")), f)
                    pts[s][0].free = [p]
                i = hp % 4
                nt, f = sums["nt"]
                d = dve(i_tensor_copy(nt.buf[:, 0, 0:32].rearrange("p (k c) -> p k c", k=4)[:, :, 2 * i:2 * i + 2],
                                      g.buf[:, 0:8].rearrange("p (k c) -> p k c", k=4)), p, f)
                g.free = [d]
                sums["t"].append(d)
                sums["y"].append(t_y)
                yield

            def scale_out(b, hf, sums):
                nt, _ = sums["nt"]
                t = dve(i_reciprocal(nt.buf[:, 1, 0:32], nt.buf[:, 0, 0:32]), sums["t"])
                r, p, t = rows(nt.buf[:, 1, 0:32], 8, t)
                nt.free = [p]
                yield
                for i in range(4):
                    hp = 4 * hf + i
                    g, p = pair_rows(r, i, t)
                    d = dve(i_tensor_tensor(AO[:, hp, :], AO[:, hp, :], g.buf[:, :], ALU.mult), p, sums["y"][i])
                    g.free = [d]
                    ao_ready[hp] = d
                    yield
                r.free = [p]

            ao_ready = {}

            def outproj(b):
                g, f = G.take()
                for i in range(8):
                    p = pe(mm(g.buf[:, :], WO[:, i, :], AO[:, i, :], i == 0, i == 7), ao_ready[i], t_w["o"], f)
                st["ao"] = p
                x0, x1 = X[0:64, b, 32:32 + L], X[64:128, b, 33:33 + L]
                d1 = dve(i_tensor_tensor(x0, g.buf[0:64, :], x0, ALU.add), p, xs_of[b][1])
                d2 = dve(i_tensor_tensor(x1, g.buf[64:128, :], x1, ALU.add), p, xs_of[b][1])
                g.free = [d1, d2]
                x_ready[b] = [d1, d2]
                wo_done[:] = [p]
                yield
                t = yield from variance(VAR[:, 0, 4 * b:4 * b + 4], X[:, b, 32:32 + L], [d1, d2], var_free)
                var_ready.append(t)

            var_ready, var_free = [], st.get("var")

            def side(b, hf):
                sums = {"nt": Nr.take(), "t": [], "y": []}
                before = None
                for i in range(4):
                    g = attend(b, 4 * hf + i, sums)
                    steps(g, 1)
                    yield
                    if before:
                        steps(before, 9)
                        yield
                    steps(g, 1)
                    yield
                    steps(g, 1)
                    before = g
                    yield
                steps(before, 9)
                yield
                yield from scale_out(b, hf, sums)
                if hf == 1:
                    st["v"] = st["v_next"]
                    yield from outproj(b)

            halves = [(b, hf) for b in range(NB) for hf in range(2)]
            run(proj(0, 0))
            run(vproj(0))
            for n, (b, hf) in enumerate(halves):
                if n + 1 < len(halves):
                    nxt = halves[n + 1]
                    run(side(b, hf), proj(*nxt))
                    if nxt[1] == 0:
                        run(vproj(nxt[0]))
                else:
                    run(side(b, hf))
            wh_done = wq_reads[-2:]

            q.phase += 1
            t_r = rsqrt(VAR, 32, var_ready)
            var_reads = []

            def ffn(b):
                g, f = G.take()
                p = pe(mm(g.buf[:, :], cmt, X[:, b, 32:32 + L]), x_ready[b], f)
                xc, f = Tr.take()
                t = act(i_copy(xc.buf[:, :], g.buf[:, :]), p, f)
                g.free = [t]
                g, p = spread(VAR[:, 3, 4 * b:4 * b + 4], t_r)
                var_reads.append(p)
                t = dve(i_tensor_tensor(xc.buf[:, :], xc.buf[:, :], g.buf[:, :], ALU.mult), t, p)
                g.free = [t]
                t = dve(i_tensor_scalar(xc.buf[:, :], xc.buf[:, :], VEC[:, layer, 0:1], VEC[:, layer, 1:2],
                                        ALU.mult, ALU.add), t, t_v)
                xs, f = Xr.take()
                t_xs = split(pool, xs.buf[0][:, 0:L], xs.buf[1][:, 0:L], xc.buf[:, :], t, f)
                xc.free = t_xs
                xh, xl = (z[:, 0:L] for z in xs.buf)
                yield
                hs = []
                for i, (o, n) in enumerate(FP):
                    ga, f = G.take()
                    pa = mm3(ga.buf[0:n, :], W1H[:, o:o + n], W1L[:, o:o + n], xh, xl, t_xs, t_w["1"], f)
                    gg, f = G.take()
                    o += F1
                    pg = mm3(gg.buf[0:n, :], W1H[:, o:o + n], W1L[:, o:o + n], xh, xl, f)
                    h, f = Tr.take()
                    a = act(i_activation(h.buf[0:n, :], gg.buf[0:n, :], ACT.Gelu, bias=VEC[0:n, layer, 5 + i:6 + i]), pg, f)
                    gg.free = [a]
                    d = dve(i_scalar_tensor_tensor(h.buf[0:n, :], ga.buf[0:n, :], VEC[0:n, layer, 2 + i:3 + i],
                                                   h.buf[0:n, :], ALU.add, ALU.mult), pa, a)
                    ga.free = [d]
                    hs.append((h, d))
                    yield
                xs.free = [pg]
                w1_reads.append(pg)
                g, f = S.take()
                for i, (o, n) in enumerate(FP):
                    p = pe(mm(g.buf[:, :], W2[0:n, i, :], hs[i][0].buf[0:n, :], i == 0, i == 2), hs[i][1], t_w["2"], f)
                for h, _ in hs:
                    h.free = [p]
                x0, x1 = X[0:64, b, 32:32 + L], X[64:128, b, 33:33 + L]
                d1 = dve(i_scalar_tensor_tensor(x0, g.buf[0:64, :], VEC[0:64, layer, 8:9], x0, ALU.add, ALU.add), p)
                d2 = dve(i_scalar_tensor_tensor(x1, g.buf[64:128, :], VEC[64:128, layer, 8:9], x1, ALU.add, ALU.add), p)
                g.free = [d1, d2]
                x_ready[b] = [d1, d2]
                w2_reads.append(p)
                yield

            w1_reads, w2_reads = [], []
            more = layer + 1 < DEPTH
            if more:
                load_wo(layer + 1)
            loader = load_split(layer + 1, [st["v"]]) if more else None
            gens = [ffn(b) for b in range(NB)]
            live = [gens.pop(0)]
            n = 0
            while live:
                for g in list(live):
                    if not steps(g):
                        live.remove(g)
                if loader:
                    steps(loader)
                n += 1
                if gens and len(live) < 2 and n >= 3:
                    live.append(gens.pop(0))
            if more:
                run(loader)
                w12_done = [w1_reads[-1], w2_reads[-1]]
                finish_w1(layer + 1)
            st["var"] = var_reads

        q.phase += 1
        outs = []

        def final(b):
            u, f = Tr.take()
            a1 = act(i_copy(u.buf[0:64, :], X[0:64, b, 32:32 + L]), x_ready[b], f)
            a2 = act(i_copy(u.buf[64:128, :], X[64:128, b, 33:33 + L]), x_ready[b])
            r, f = Tr.take()
            t_r = dma(r.buf[:, :], x1d[:, b, :], f"x{b % 2}", x1_store[b], f)
            yield
            xc, gr, t = yield from norm(u.buf[:, :], [a1, a2])
            m = dve(i_tensor_tensor(xc.buf[:, :], xc.buf[:, :], gr.buf[:, :], ALU.mult), t)
            gr.free = [m]
            m = pool(i_tensor_tensor(r.buf[:, :], r.buf[:, :], xc.buf[:, :], ALU.add), m, t_r)
            xc.free = [m]
            yield
            g, f = G.take()
            for i in range(4):
                p = pe(i_transpose(g.buf[:, 128 * i:128 * i + 128], r.buf[:, 128 * i:128 * i + 128], ident), m, f)
            a = act(i_copy(u.buf[:, :], g.buf[:, :]), p)
            g.free = [a]
            r.free = [p]
            t = dma(out[b].rearrange("(a p) d -> p a d", p=128), u.buf[:, :].rearrange("p (a d) -> p a d", a=4), f"o{b}", a)
            u.free = [t]
            outs.append(t)
            yield

        for b in range(0, NB, 2):
            run(final(b), final(b + 1))
        op("sp", None, outs, x1_store)

        q.number(lambda n: ctx.enter_context(nc.semaphore(n)))
        block = ctx.enter_context(nc.Block())

        @block.sync
        def _(e):
            q.emit("sp", e)

        @block.tensor
        def _(e):
            q.emit("pe", e)

        @block.vector
        def _(e):
            q.emit("dve", e)

        @block.scalar
        def _(e):
            q.emit("act", e)

        @block.gpsimd
        def _(e):
            q.emit("pool", e)


def kernel(**inputs):
    import numpy as _np
    import concourse.bacc as _bacc
    from concourse import mybir as _mybir
    from concourse.bass_utils import run_bass_kernel_spmd as _run

    g = {k: _np.asarray(v) for k, v in inputs.items()}
    vec = _np.zeros((128, DEPTH, 16), _np.float32)
    for l in range(DEPTH):
        vec[:, l, 0] = g["L0_ffn_ln_g"][l]
        vec[:, l, 1] = g["L0_ffn_ln_b"][l]
        for i, (o, n) in enumerate(FP):
            vec[0:n, l, 2 + i] = g["L0_ffn_b1"][l, o:o + n]
            vec[0:n, l, 5 + i] = g["L0_ffn_b1"][l, F1 + o:F1 + o + n]
        vec[:, l, 8] = g["L0_ffn_b2"][l]
        for i, n in enumerate(("L0_ffn_q_scale", "L0_ffn_k_scale")):
            s = g[n][l]
            for h in range(2):
                vec[64 * h:64 * h + 64, l, 9 + 2 * i] = s
                vec[64 * h:64 * h + 32, l, 10 + 2 * i] = s[32:64]
                vec[64 * h + 32:64 * h + 64, l, 10 + 2 * i] = s[0:32]
        for h in range(2):
            vec[64 * h:64 * h + 64, l, 13] = g["L0_attn_g_weight"]
    wo = _np.ascontiguousarray(g["L0_attn_Wo"].T.reshape(8, 128, 128).transpose(1, 0, 2).reshape(128, 1024))
    data = [
        ("x", g["L0_attn_hidden_states"]), ("cst", constants()),
        ("awq", g["L0_attn_Wq"].T), ("awk", g["L0_attn_Wk"].T), ("awv", g["L0_attn_Wv"].T), ("awo", wo),
        ("wqkv", g["L0_ffn_Wqkv"]), ("wo", g["L0_ffn_Wo"]), ("w1", g["L0_ffn_W1"]), ("w2", g["L0_ffn_W2"]), ("vec", vec),
    ]
    nc = _bacc.Bacc("TRN2", target_bir_lowering=False, num_devices=1)
    arrays, args = {}, []
    for name, a in data:
        a = _np.ascontiguousarray(a)
        arrays["in_" + name] = a
        args.append(nc.dram_tensor("in_" + name, a.shape, _mybir.dt.from_np(a.dtype), kind="ExternalInput").ap())
    o = nc.dram_tensor("out_0", (NB, L, D), F32, kind="ExternalOutput").ap()
    build(nc, *args, o)
    r = _run(nc, [arrays], core_ids=[0])
    return r.results[0]["out_0"]
```

```python
from contextlib import ExitStack

import numpy as np
import concourse.bass as bass
from concourse import mybir

F32 = mybir.dt.float32
F32R = mybir.dt.float32r
BF16 = mybir.dt.bfloat16
ACT = mybir.ActivationFunctionType
ALU = mybir.AluOpType
AX_X = mybir.AxisListType.X

NB, L, D = 8, 512, 128
DEPTH = 6
F1 = 341
FP = [(0, 114), (114, 114), (228, 113)]
EPS = 1e-5
NEG = -1.0e30

CONST = {}
CONST_COLS = 0
for _n, _w in (("ident", 128), ("cm", 128), ("om", 1), ("one", 1), ("tri", 128), ("hsel", 64), ("ssel", 64), ("cum", 12),
               ("mske", 16), ("hilo", 3), ("tab", 2048), ("nsel", 256), ("bsel", 1024), ("mask", 480), ("kneg", 288)):
    CONST[_n] = (CONST_COLS, _w)
    CONST_COLS += _w
KEPT = CONST["nsel"][0]


def constants():
    c = np.zeros((128, CONST_COLS), np.float32)

    def part(n):
        o, w = CONST[n]
        return c[:, o:o + w]

    eye = np.eye(128, dtype=np.float32)
    part("ident")[:] = eye
    part("cm")[:] = eye - np.float32(1.0 / 128)
    part("om")[:] = 1.0 / 128
    r = np.arange(128)
    part("one")[:] = 1.0
    part("tri")[:] = r[:, None] <= r[None, :]
    for i in range(2):
        part("ssel")[:, 32 * i:32 * i + 32] = (r[:, None] // 64 + i) % 2 == np.arange(32)[None, :] % 2
    for k in range(2):
        for base in (0, 16):
            for s in range(2):
                part("hsel")[64 * s:64 * s + 64, 32 * k + base + 2 * k + s] = 1.0
    for j in range(3):
        for i in range(4):
            part("cum")[:, 4 * j + i] = float(i > j)
    for p in range(32):
        part("mske")[p, p % 16] = 1.0
        for i in range(2):
            o = 128 * i + 64 * ((p // 16 + p % 16 // 2 + i) % 2)
            part("nsel")[p, o:o + 64] = -1.0
            part("kneg")[i, p] = (p // 16 + p % 16 // 2) % 2 == i
        part("kneg")[2, p] = p % 2
    part("hilo")[:, 0] = -1.0 * (r % 64 // 16 == 1)
    part("hilo")[:, 1] = -1.0 * (r % 64 // 16 == 2)
    part("hilo")[:, 2] = -1.0 * (r % 32 >= 16)
    for i in range(8):
        for s in range(2):
            for base in (0, 16):
                part("bsel")[32 * (i % 4) + 2 * (i // 4) + s + base, 128 * i + 64 * s:128 * i + 64 * s + 64] = 1.0
    half = np.arange(0, 64, 2, dtype=np.float32)
    inv_freq = (1.0 / np.float32(10000.0) ** (half / np.float32(64))).astype(np.float32)
    t = np.arange(L, dtype=np.float32)
    freqs = (t[:, None] * inv_freq[None, :]).astype(np.float32)
    base = ((half + 0.4 * 64) / (1.4 * 64)).astype(np.float64)
    power = (np.arange(L) - L // 2) / 16.0
    scale = base[None, :] ** power[:, None]
    cos, sin = np.cos(freqs.astype(np.float64)), np.sin(freqs.astype(np.float64))
    sgn = np.where(np.arange(64) < 32, 1.0, -1.0)

    def dims(a):
        return np.concatenate([a, a], 1)

    tabs = [dims(cos * scale) * 8.0, dims(sin * scale) * sgn * 8.0, dims(cos / scale), dims(sin / scale) * sgn]
    for i, a in enumerate(tabs):
        part("tab")[:, 512 * i:512 * i + 512] = np.concatenate([a.T, a.T], 0)
    d = np.arange(96)[None, :] - (r % 64)[:, None]
    m = np.tile(np.where((d >= 0) & (d <= 32), 0.0, NEG), (1, 5))
    for i in range(2):
        part("kneg")[i, 32 + 64 * (1 - i):96 + 64 * (1 - i)] = NEG
        part("kneg")[i, 160 + 64 * i:224 + 64 * i] = NEG
    part("kneg")[2, 160:288] = NEG
    part("mask")[:] = m
    return c


class Tok:

    def __init__(self, eng):
        self.eng, self.used, self.sem, self.val = eng, False, None, 0


class Queues:

    def __init__(self):
        self.q = {e: [] for e in ("pe", "act", "dve", "pool", "sp")}
        self.phase = 0

    def op(self, eng, fn, *after, sem=None):
        tok = Tok(eng)
        flat = []
        for a in after:
            flat += a if isinstance(a, list) else [a]
        flat = [a for a in flat if a is not None]
        for a in flat:
            a.used = True
        self.q[eng].append((fn, flat, tok, sem, self.phase))
        return tok

    def number(self, new_sem):
        sems, counts = {}, {}
        for eng, ops in self.q.items():
            for fn, after, tok, sem, phase in ops:
                if sem is None and not tok.used:
                    continue
                key = sem if sem is not None else (eng, phase)
                if key not in sems:
                    sems[key] = new_sem("s_" + "_".join(str(x) for x in (key if isinstance(key, tuple) else (key,))))
                    counts[key] = 0
                counts[key] += 16 if sem is not None else 1
                tok.sem, tok.val = sems[key], counts[key]
                tok.key = key

    def emit(self, eng, e):
        seen = {}
        for fn, after, tok, sem, phase in self.q[eng]:
            for a in after:
                if seen.get(a.key, 0) < a.val:
                    e.wait_ge(a.sem, a.val)
                    seen[a.key] = a.val
            if fn is None:
                continue
            ins = fn(e)
            if tok.sem is not None:
                ins.then_inc(tok.sem, 16 if sem is not None else 1)


class Slot:

    def __init__(self, buf, ring=None):
        self.buf, self.ring, self.after, self.n = buf, ring, [], 0

    @property
    def free(self):
        return self.after

    @free.setter
    def free(self, toks):
        self.after = toks
        if self.ring is not None:
            assert self not in self.ring, "given back twice"
            self.ring.append(self)


class Ring:

    def __init__(self, bufs):
        self.idle = []
        for n, b in enumerate(bufs):
            s = Slot(b, self.idle)
            s.n = n
            self.idle.append(s)

    def take(self):
        assert self.idle, "every buffer is in use"
        s = self.idle.pop(0)
        return s, s.after


def i_activation(*a, **k):
    return lambda e: e.activation(*a, **k)


def i_copy(*a, **k):
    return lambda e: e.copy(*a, **k)


def i_memset(*a, **k):
    return lambda e: e.memset(*a, **k)


def i_reciprocal(*a, **k):
    return lambda e: e.reciprocal(*a, **k)


def i_scalar_tensor_tensor(*a, **k):
    return lambda e: e.scalar_tensor_tensor(*a, **k)


def i_tensor_copy(*a, **k):
    return lambda e: e.tensor_copy(*a, **k)


def i_tensor_reduce(*a, **k):
    return lambda e: e.tensor_reduce(*a, **k)


def i_tensor_scalar(*a, **k):
    return lambda e: e.tensor_scalar(*a, **k)


def i_tensor_tensor(*a, **k):
    return lambda e: e.tensor_tensor(*a, **k)


def i_transpose(*a, **k):
    return lambda e: e.transpose(*a, **k)


def mm(o, lhsT, rhs, start=True, stop=True, **kw):
    return lambda e: e.matmul(o, lhsT, rhs, start=start, stop=stop, **kw)


def run(*gens):
    gens = list(gens)
    while gens:
        for g in list(gens):
            if not steps(g):
                gens.remove(g)


def until(g):
    for mark in g:
        if mark:
            return
        yield


def steps(g, n=1):
    for _ in range(n):
        try:
            next(g)
        except StopIteration:
            return False
    return True


def build(nc, xin, cst, awq, awk, awv, awo, wqkv, wo, w1, w2, vec, out):
    with ExitStack() as ctx:
        def sb(name, shape, dt=F32, c=ctx):
            return c.enter_context(nc.sbuf_tensor(name, shape, dt))

        x1d = nc.dram_tensor("x1_scratch", (128, NB, L), F32, kind="Internal").ap()
        bank = [ctx.enter_context(nc.psum_tensor(f"bank{i}", [128, 512], F32)) for i in range(8)]
        X = sb("X", [128, NB, L + 1])
        C = sb("C", [128, KEPT])
        WH = sb("WH", [128, 3072], F32R)
        WL = sb("WL", [128, 3072], F32R)
        WO = sb("WO", [128, 8, 128])
        W1H = sb("W1H", [128, 2 * F1], F32R)
        W1L = sb("W1L", [128, 2 * F1], F32R)
        W2 = sb("W2", [128, 3, 128])
        VEC = sb("VEC", [128, DEPTH, 16])
        VB = sb("VB", [128, 9, 512])
        AO = sb("AO", [128, 8, L])
        nselr = sb("nselr", [32, 256], F32R)
        bselr = sb("bselr", [128, 1024], F32R)
        identb = sb("identb", [128, 128], BF16)
        maskb = sb("maskb", [128, 480], BF16)
        knegb = sb("knegb", [3, 288], BF16)
        cumt = sb("cumt", [128, 32])
        VAR = sb("VAR", [128, 4, 32])
        Tr = Ring([sb(f"T{i}", [128, L]) for i in range(14)])
        Qr = Ring([sb(f"sq{i}", [128, L]) for i in range(5)])
        Rr = Ring([sb(f"R{i}", [128, L], F32R) for i in range(2)])
        Xr = Ring([(sb(f"XH{i}", [128, L + 64], F32R), sb(f"XL{i}", [128, L + 64], F32R)) for i in range(2)])
        Er = Ring([sb(f"E{i}", [32, L], F32R) for i in range(2)])
        Pr = Ring([sb(f"P{i}", [128, 736]) for i in range(5)])
        Mt = [sb(f"M{i}", [128, 96]) for i in range(3)]
        Mr = Ring(Mt)
        Nr = Ring([sb(f"N{i}", [128, 4, 4]) for i in range(3)])
        with ExitStack() as ca:
            QA = sb("QA", [128, 8, L], F32R, ca)
            KA = sb("KA", [128, 8, L], F32R, ca)
        Q = sb("Q", [128, 8, L])
        K = sb("K", [128, 8, L])
        G = Ring(bank[0:2])
        S = Ring(bank[2:5])
        yb, ssb, smb = Slot(bank[5]), Slot(bank[6]), Slot(bank[7])
        Vf = VB[:, :, :].rearrange("p a b -> p (a b)")
        V = Vf[:, 0:4096].rearrange("p (a b) -> p a b", a=4)
        Vj = VB[:, :, :].rearrange("p j (h d) -> p j h d", d=64)
        AOf = AO[:, :, :].rearrange("p a b -> p (a b)")

        def cn(n, rows=128):
            o, w = CONST[n]
            return C[0:rows, o:o + w]

        q = Queues()
        op = q.op

        def pe(fn, *a):
            return op("pe", fn, *a)

        def act(fn, *a):
            return op("act", fn, *a)

        def dve(fn, *a):
            return op("dve", fn, *a)

        def pool(fn, *a):
            return op("pool", fn, *a)

        def dma(o, i, key, *a):
            return op("sp", lambda e: e.dma_start(o, i), *a, sem=key)

        def split(eng, hi, lo, src, *a):
            t1 = act(i_copy(hi, src), *a)
            t2 = eng(i_tensor_tensor(lo, src, hi.bitcast(F32), ALU.subtract), t1)
            return [t1, t2]

        def mm3(o, lh, ll, rh, rl, *a):
            pe(mm(o, lh, rh, True, False), *a)
            pe(mm(o, lh, rl, False, False), *a)
            return pe(mm(o, ll, rh, False, True), *a)

        t_c = dma(C[:, :], cst[:, 0:KEPT], "c")
        t_v = dma(VEC[:, :, :], vec, "v")
        n_sel = CONST_COLS - KEPT
        t_s = dma(Vf[:, 0:n_sel], cst[:, KEPT:CONST_COLS], "c2")
        t_aq = dma(Vf[:, 2304:2560], awq, "w0")
        t_ak = dma(Vf[:, 2560:2816], awk, "w1")
        t_av = dma(Vf[:, 2816:3840], awv, "w2")
        t_ao = dma(WO[:, :, :], awo.rearrange("p (c d) -> p c d", c=8), "w3")
        z1 = [pool(i_memset(m[:, 0:1], NEG)) for m in Mt]
        z2b = [pool(i_memset(z[:, 0:64].bitcast(F32), 0.0)) for x in Xr.idle for z in x.buf]
        z0 = pool(i_memset(X[:, :, 0:1], 0.0))
        z2 = pool(i_memset(AOf[:, 0:2048], 0.0))
        act(lambda e: e.preload_act_table_set("natural_log_exp_and_others"))
        c1 = dve(i_tensor_copy(nselr[:, :], Vf[0:32, 0:256]), t_s)
        c2 = dve(i_tensor_copy(bselr[:, :], Vf[:, 256:1280]), t_s)
        c4 = dve(i_tensor_copy(maskb[:, :], Vf[:, 1280:1760]), t_s)
        c5 = dve(i_tensor_copy(knegb[:, :], Vf[0:3, 1760:2048]), t_s)
        c3 = dve(i_tensor_copy(identb[:, :], cn("ident")), t_c)
        t_wa = []
        for n, tw in ((0, t_aq), (1, t_ak)):
            dst = AOf[:, 1024 * n:1024 + 1024 * n].rearrange("p (h c) -> p h c", c=64)
            src = Vf[:, 2304 + 256 * n:2560 + 256 * n].rearrange("p (h c) -> p h c", c=16)
            cp = [pool(i_tensor_copy(dst[:, :, 16 * i:16 * i + 16], src), tw, z2) for i in range(3)]
            for i in range(2):
                a = 1024 * n + 512 * i
                t_wa += split(dve, WH[:, a:a + 512], WL[:, a:a + 512], AOf[:, a:a + 512], cp)
        for i in range(2):
            t_wa += split(dve, WH[:, 2048 + 512 * i:2560 + 512 * i], WL[:, 2048 + 512 * i:2560 + 512 * i],
                          Vf[:, 2816 + 512 * i:3328 + 512 * i], t_av)
        stage_read = [c1, c2, c4, c5] + t_wa
        ident = cn("ident")
        cmt = cn("cm")

        def rsqrt(nt, n, *a):
            v, r, u, w = (nt[:, i, 0:n] for i in range(4))
            t = act(i_activation(u, v, ACT.Ln), *a)
            t = act(i_activation(r, u, ACT.Exp, scale=-0.5), t)
            t = dve(i_tensor_tensor(u, v, r, ALU.mult), t)
            t = dve(i_scalar_tensor_tensor(u, u, -0.5, r, ALU.mult, ALU.mult), t)
            return dve(i_scalar_tensor_tensor(w, u, 1.5, r, ALU.add, ALU.mult), t)

        def spread(src, *a):
            g, f = G.take()
            for k in range(4):
                p = pe(mm(g.buf[:, 128 * k:128 * k + 128], src[:, k:k + 1].broadcast_to([128, 128]), ident), *a, f)
            return g, p

        def variance(dst, src, *a, keep=None):
            g, f = G.take()
            p = pe(mm(g.buf[:, :], cmt, src), *a, f, t_c)
            sq, f = Qr.take()
            t_sq = act(i_activation(sq.buf[:, :], g.buf[:, :], ACT.Square), p, f)
            g.free = [t_sq]
            if keep is not None:
                g.after += keep_copy(keep, g)
            yield
            g2, f = G.take()
            for k in range(4):
                p = pe(mm(g2.buf[:, k:k + 1], sq.buf[:, 128 * k:128 * k + 128], cn("om")), t_sq, f)
            sq.free = [p]
            t = dve(i_tensor_scalar(dst, g2.buf[:, 0:4], EPS, None, ALU.add), p, *a)
            g2.free = [t]
            yield
            return t

        def keep_copy(keep, g):
            keep["t"] = act(i_copy(keep["xc"].buf[:, :], g.buf[:, :]), keep["f"])
            return [keep["t"]]

        def norm(src, *a):
            nt, f1 = Nr.take()
            xc, f2 = Tr.take()
            keep = {"xc": xc, "f": f2}
            t = yield from variance(nt.buf[:, 0, 0:4], src, *a, f1, keep=keep)
            t = rsqrt(nt.buf, 4, t)
            yield
            gr, p = spread(nt.buf[:, 3, 0:4], t)
            nt.free = [p]
            return xc, gr, [keep["t"], p]

        def row_sums(slot, tiles, k, *a):
            for c, (t, tok) in enumerate(tiles):
                p = pe(mm(slot.buf[32 * c:32 * c + 32, :], cn("hsel")[:, 32 * k:32 * k + 32], t.buf[:, :], k == 0, k == 1),
                       [x[1] for x in tiles], *a, t_c)
            return p

        def two_parts(w, t):
            h, f = Tr.take()
            t1 = act(i_copy(h.buf[:, :].bitcast(F32R), w.buf[:, :]), t, f)
            r, f = Rr.take()
            t2 = dve(i_scalar_tensor_tensor(r.buf[:, :], h.buf[:, :], cn("hilo")[:, 2:3], w.buf[:, :], ALU.mult, ALU.add), t1, f)
            h.free = [t2]
            w.free = [t2]
            return r, t2

        def inverse_roots(slot, op0, s0, op1, s1, p, between=None):
            v, f = Tr.take()
            t = dve(i_tensor_scalar(v.buf[:, :], slot.buf[:, :], s0, s1, op0, op1) if op1 is not None else
                    i_tensor_scalar(v.buf[:, :], slot.buf[:, :], s0, None, op0), p, f)
            slot.free = [t]
            u, f = Tr.take()
            t = act(i_activation(u.buf[:, :], v.buf[:, :], ACT.Ln), t, f)
            r, f = Tr.take()
            t = act(i_activation(r.buf[:, :], u.buf[:, :], ACT.Exp, scale=-0.5), t, f)
            yield
            if between:
                between()
            t = dve(i_tensor_tensor(u.buf[:, :], v.buf[:, :], r.buf[:, :], ALU.mult), t)
            v.free = [t]
            t = dve(i_scalar_tensor_tensor(u.buf[:, :], u.buf[:, :], -0.5, r.buf[:, :], ALU.mult, ALU.mult), t)
            t = dve(i_scalar_tensor_tensor(r.buf[:, :], u.buf[:, :], 1.5, r.buf[:, :], ALU.add, ALU.mult), t)
            u.free = [t]
            yield
            return two_parts(r, t)

        def inverses(slot, p):
            u, f = Tr.take()
            t = act(i_activation(u.buf[:, :], slot.buf[:, :], ACT.Ln), p, f)
            r, f = Tr.take()
            t = act(i_activation(r.buf[:, :], u.buf[:, :], ACT.Exp, scale=-1.0), t, f)
            yield
            t = dve(i_scalar_tensor_tensor(u.buf[:, :], slot.buf[:, :], -1.0, r.buf[:, :], ALU.mult, ALU.mult), t)
            slot.free = [t]
            t = dve(i_scalar_tensor_tensor(r.buf[:, :], u.buf[:, :], 2.0, r.buf[:, :], ALU.add, ALU.mult), t)
            u.free = [t]
            yield
            return two_parts(r, t)

        def pair_rows(r, i, *a):
            g, f = G.take()
            return g, pe(mm(g.buf[:, :], bselr[:, 128 * i:128 * i + 128], r.buf[:, :]), c2, *a, f)

        x_ready = [None] * NB
        x1_store = [None] * NB
        xa_of, xs_of, v_of = {}, {}, {}
        sa = {"v": stage_read, "ao": t_wa, "cum": None, "k": [None] * 8}
        qa_ready = {}

        def a_load(b):
            s0, f = Tr.take()
            t_x = dma(s0.buf[:, :].rearrange("p (a d) -> p a d", a=4), xin[b].rearrange("(a p) d -> p a d", p=128),
                      f"x{b % 2}", f)
            g, f = G.take()
            for i in range(4):
                p = pe(i_transpose(g.buf[:, 128 * i:128 * i + 128], s0.buf[:, 128 * i:128 * i + 128], ident), t_x, t_c, f)
            xa, f = Tr.take()
            s0.free = [p]
            t_xa = act(i_copy(xa.buf[:, :], g.buf[:, :]), p, f)
            g.free = [t_xa]
            xa_of[b] = (xa, t_xa)
            yield
            xc, gr, t = yield from norm(xa.buf[:, :], t_xa)
            t_xn = dve(i_tensor_tensor(xc.buf[:, :], xc.buf[:, :], gr.buf[:, :], ALU.mult), t)
            gr.free = [t_xn]
            xs, f = Xr.take()
            t = split(pool, xs.buf[0][:, 64:], xs.buf[1][:, 64:], xc.buf[:, :], t_xn, f)
            xc.free = t
            xs_of[b] = (xs, t)
            yield

        def a_qk(b, hf):
            xs, t_xs = xs_of[b]
            xh, xl = (z[:, 64:] for z in xs.buf)
            for hp in range(4 * hf, 4 * hf + 4):
                toks = []
                for n, dst in ((0, QA), (1, KA)):
                    c = slice(1024 * n + 128 * hp, 1024 * n + 128 * hp + 128)
                    g, f = G.take()
                    p = mm3(g.buf[:, :], WH[:, c], WL[:, c], xh, xl, t_xs, t_wa, f)
                    h, f = Tr.take()
                    t = act(i_copy(h.buf[:, :].bitcast(F32R), g.buf[:, :]), p, f)
                    t = dve(i_scalar_tensor_tensor(dst[:, hp, :], h.buf[:, :], cn("hilo")[:, n:n + 1], g.buf[:, :],
                                                   ALU.mult, ALU.add), t, sa["k"][hp])
                    g.free = [t]
                    h.free = [t]
                    toks.append(t)
                    yield
                qa_ready[(b, hp)] = toks

        def a_v(b):
            xs, t_xs = xs_of[b]
            xh, xl = (z[:, 64:] for z in xs.buf)
            toks = []
            for i in range(4):
                for n in range(2):
                    c = slice(2048 + 512 * n, 2560 + 512 * n)
                    k = slice(128 * i, 128 * i + 128)
                    g, f = G.take()
                    p = mm3(g.buf[:, :], xh[:, k], xl[:, k], WH[:, c], WL[:, c], t_xs, t_wa, f)
                    t = act(i_copy(V[:, i, 512 * n:512 * n + 512], g.buf[:, :]), p, sa["v"])
                    g.free = [t]
                    toks.append(t)
                yield
            xs.free = [p]
            g, f = G.take()
            for h in range(8):
                for j in range(3):
                    p = pe(mm(g.buf[:, 4 * h:4 * h + 4], V[:, j, 128 * h:128 * h + 128], cn("cum")[:, 4 * j:4 * j + 4],
                              h == 0 and j == 0, h == 7 and j == 2, skip_group_check=True), toks, f)
            t = dve(i_tensor_copy(cumt[:, :], g.buf[:, 0:32]), p, sa["cum"])
            g.free = [t]
            v_of[b] = (toks, t)
            yield

        def a_attend(b):
            t_v_ready, t_cum = v_of[b]
            t_y, ss = [], []
            f_ss = ssb.free
            for hp in range(8):
                f_y = yb.free
                for j in range(4):
                    pts = []
                    n = L - 128 * j
                    for s in range(2):
                        st, f = S.take()
                        r0 = 64 * s
                        p = pe(mm(st.buf[:, 0:n], KA[r0:r0 + 64, hp, 128 * j:128 * j + 128], QA[r0:r0 + 64, hp, 128 * j:512]),
                               qa_ready[(b, hp)], f)
                        pt, f = Pr.take()
                        t = act(i_activation(pt.buf[:, 0:n], st.buf[:, 0:n], ACT.Square, bias=1.0, scale=0.25), p, f)
                        st.free = [t]
                        t2 = dve(i_scalar_tensor_tensor(pt.buf[:, 0:128], pt.buf[:, 0:128], 1.0, cn("tri"),
                                                        ALU.add, ALU.mult), t)
                        pts.append((pt, [t, t2]))
                    if j == 3:
                        sa["k"][hp] = p
                    yield
                    for s in range(2):
                        h = 2 * hp + s
                        pt, tt = pts[s]
                        p2 = pe(mm(yb.buf[64 * s:64 * s + 64, 128 * j:512], V[:, j, 64 * h:64 * h + 64], pt.buf[:, 0:n],
                                   j == 0, j == 3), tt, t_v_ready, f_y)
                    for s in range(2):
                        pts[s][0].free = [p2]
                cb = cumt[:, 4 * hp:4 * hp + 4].rearrange("p (a o) -> p a o", o=1).broadcast_to([128, 4, 128])
                d = dve(i_tensor_tensor(AO[:, hp, :].rearrange("p (a c) -> p a c", a=4),
                                        yb.buf[:, :].rearrange("p (a c) -> p a c", a=4), cb, ALU.add), p2, t_cum, sa["ao"])
                yb.free = [d]
                sq, f = Qr.take()
                a = act(i_activation(sq.buf[:, :], AO[:, hp, :], ACT.Square), d, f)
                ss.append((sq, a))
                t_y.append(d)
                yield
                if hp % 4 == 3:
                    p = row_sums(ssb, ss, hp // 4, f_ss)
                    for sq, _ in ss:
                        sq.free = [p]
                    ss = []
                if hp == 3:
                    yield True
            sa["v"] = p2
            sa["cum"] = t_y[-1]
            r, t = yield from inverse_roots(ssb, ALU.mult, 1.0 / 64, ALU.add, 4 * EPS, p)
            yield
            for hp in range(8):
                g, p = pair_rows(r, hp, t)
                t2 = dve(i_scalar_tensor_tensor(AO[:, hp, :], AO[:, hp, :], VEC[:, 0, 13:14], g.buf[:, :], ALU.mult, ALU.mult),
                         p, t_v, t_y[hp])
                g.free = [t2]
                t_y[hp] = t2
                if hp % 2:
                    yield
            r.free = [p]
            sa["y"] = t_y

        def a_out(b):
            xa, t_xa = xa_of.pop(b)
            g, f = G.take()
            for i in range(8):
                p = pe(mm(g.buf[:, :], WO[:, i, :], AO[:, i, :], i == 0, i == 7), sa["y"][i], t_ao, f)
            sa["ao"] = sa["wo"] = p
            z, f = Tr.take()
            t_z = act(i_copy(z.buf[:, :], g.buf[:, :]), p, f)
            g.free = [t_z]
            yield
            xc, gr, t = yield from norm(z.buf[:, :], t_z)
            m = dve(i_tensor_tensor(z.buf[:, :], xc.buf[:, :], gr.buf[:, :], ALU.mult), t)
            xc.free = [m]
            gr.free = [m]
            t_x1 = pool(i_tensor_tensor(xa.buf[:, :], xa.buf[:, :], z.buf[:, :], ALU.add), m, t_xa)
            x1_store[b] = dma(x1d[:, b, :], xa.buf[:, :], f"x1s{b}", t_x1)
            z.free = [t_x1]
            yield
            xc, gr, t = yield from norm(xa.buf[:, :], t_x1)
            xa.free = [x1_store[b], t[1]]
            m1 = dve(i_tensor_tensor(X[0:64, b, 0:L], xc.buf[0:64, :], gr.buf[0:64, :], ALU.mult), t, z0)
            m2 = dve(i_tensor_tensor(X[64:128, b, 1:1 + L], xc.buf[64:128, :], gr.buf[64:128, :], ALU.mult), t, z0)
            xc.free = [m1, m2]
            gr.free = [m1, m2]
            x_ready[b] = [m1, m2]
            yield

        def a_next(b):
            yield from a_load(b)
            yield from a_qk(b, 0)

        run(a_next(0))
        run(a_v(0))
        for b in range(NB):
            att = a_attend(b)
            gens = []
            if b:
                gens = [a_out(b - 1)]
                steps(gens[0], 1)
            run(until(att), a_qk(b, 1), *gens)
            run(att, *([a_next(b + 1)] if b + 1 < NB else []))
            if b + 1 < NB:
                run(a_v(b + 1))
        run(a_out(NB - 1))
        end_a = sa["v"]
        wh_done = [v_of[NB - 1][1], sa["v"]]

        def phase_slots():
            out, S.idle[:] = sorted(S.idle, key=lambda x: x.n), []
            return out

        def end_slots(slots):
            S.idle.extend(slots)

        st = {"k": [end_a] * 8, "ao": [sa["wo"]] * 2}
        wo_done, w12_done = [sa["wo"]], []

        def load_split(layer, stage_free):
            t = dma(Vf[:, 0:3072], wqkv[layer], "w4", stage_free)
            t_w["1d"] = dma(Vf[:, 3072:3072 + 2 * F1], w1[layer], "w6", stage_free)
            toks = []
            for c in range(0, 3072, 512):
                toks += split(dve, WH[:, c:c + 512], WL[:, c:c + 512], Vf[:, c:c + 512], t, wh_done)
                yield
            t_w["qkv"] = toks

        def finish_w1(layer):
            t_w["1"] = split(dve, W1H[:, :], W1L[:, :], Vf[:, 3072:3072 + 2 * F1], t_w["1d"], w12_done)
            t_w["2"] = [dma(W2[0:n, i, :], w2[layer, o:o + n, :], f"w{7 + i}", w12_done) for i, (o, n) in enumerate(FP)]

        def load_wo(layer):
            t_w["o"] = dma(WO[:, :, :], wo[layer].rearrange("(c p) d -> p c d", p=128), "w5", wo_done)

        t_w = {}
        run(load_split(0, [sa["v"]]))
        finish_w1(0)
        load_wo(0)
        for layer in range(DEPTH):
            q.phase += 1
            v_ready, qk_ready, wq_reads = {}, {}, []
            t_wq = t_w["qkv"]
            if layer:
                act(lambda e: e.preload_act_table_set("natural_log_exp_and_others"))
            st["v"] = [t_w["1"] + t_wq] * 2
            tb = CONST["tab"][0]

            def xsplit(b):
                xs, f = Xr.take()
                t = split(pool, xs.buf[0][:, 64:], xs.buf[1][:, 64:], X[:, b, 0:L], x_ready[b], f)
                xs_of[b] = (xs, t)

            def vproj(b, hf):
                xs, t_xs = xs_of[b]
                xh, xl = xs.buf
                wh, wl = (w[:, 2048 + 512 * hf:2560 + 512 * hf].rearrange("p (i s d) -> p s i d", i=4, s=2) for w in (WH, WL))
                toks = []
                for c in range(5):
                    g, f = G.take()
                    m = 128 if c < 4 else 64
                    for s in ((0, 1) if c < 4 else (1,)):
                        k = slice(128 * c + 64 - 64 * s, 128 * c + 64 - 64 * s + m)
                        o = 256 * s if c < 4 else 0
                        p = mm3(g.buf[0:m, o:o + 256], xh[:, k], xl[:, k], wh[:, s], wl[:, s], t_wq, t_xs, z2b, f)
                    n = 2 if c < 4 else 1
                    a = act(i_copy(Vj[0:m, 2 * c:2 * c + n, 4 * hf:4 * hf + 4, :],
                                   g.buf[0:m, 0:256 * n].rearrange("p (a h d) -> p a h d", a=n, d=64)), p, st["v"][hf])
                    g.free = [a]
                    toks.append(a)
                    if c == 4:
                        v_ready[(b, hf)] = toks
                        wq_reads.append(p)
                        if hf == 1:
                            xs.free = [p]
                    if c != 3:
                        yield

            def add(pr, least=1):
                if len(pr["adds"]) < least:
                    return
                dst, t1, t3, d1, tok, hp = pr["adds"].pop(0)
                r = pool(i_tensor_tensor(dst, t1.buf[:, :], t3.buf[:, :], ALU.add), d1, tok, st["k"][hp])
                t1.free = [r]
                t3.free = [r]
                pr["raw"].append(r)

            def proj(b, hf, pr):
                xs, t_xs = xs_of[b]
                xh, xl = (z[:, 64:] for z in xs.buf)
                ss = []

                def sums(k):
                    p = row_sums(ssb, ss[0:4], k, f_ss)
                    for x, _ in ss[0:4]:
                        x.free = [p]
                    del ss[0:4]
                    return p

                for i in range(4):
                    hp = 4 * hf + i
                    for w in range(2):
                        c = slice(1024 * w + 128 * hp, 1024 * w + 128 * hp + 128)
                        g, f = G.take()
                        p = mm3(g.buf[:, :], WH[:, c], WL[:, c], xh[:, :], xl[:, :], t_wq, t_xs, f)
                        t1, f = Tr.take()
                        a = act(i_copy(t1.buf[:, :], g.buf[:, :]), p, f)
                        g.free = [a]
                        sq, f = Qr.take()
                        a2 = act(i_activation(sq.buf[:, :], t1.buf[:, :], ACT.Square), a, f)
                        ss.append((sq, a2))
                        scl = VEC[:, layer, 9 + w:10 + w]
                        o = tb + 1024 * w
                        t2, f = Tr.take()
                        d2 = dve(i_scalar_tensor_tensor(t2.buf[:, :], t1.buf[:, :], scl, C[:, o + 512:o + 1024],
                                                        ALU.mult, ALU.mult), a, t_c, t_v, f)
                        d1 = dve(i_scalar_tensor_tensor(t1.buf[:, :], t1.buf[:, :], scl, C[:, o:o + 512],
                                                        ALU.mult, ALU.mult), a2)
                        t3, f = Tr.take()
                        for x in range(4):
                            y = x ^ 1
                            tok = dma(t3.buf[32 * x:32 * x + 32, :], t2.buf[32 * y:32 * y + 32, :], f"t{t3.n}", d2, f)
                        t2.free = [tok]
                        pr["adds"].append((Q[:, hp, :] if w == 0 else K[:, hp, :], t1, t3, d1, tok, hp))
                        if i == 2 and w == 0:
                            f_ss = ssb.free
                            sums(0)
                        yield
                wq_reads.append(p)
                p = sums(1)
                r, t = yield from inverse_roots(ssb, ALU.max, 1e-24, None, None, p)
                yield
                for i in range(4):
                    hp = 4 * hf + i
                    fin = []
                    while len(pr["raw"]) < 2 * i + 2:
                        add(pr)
                    for w in range(2):
                        g, p = pair_rows(r, 2 * i + w, t)
                        dst = Q[:, hp, :] if w == 0 else K[:, hp, :]
                        d = dve(i_tensor_tensor(dst, dst, g.buf[:, :], ALU.mult), p, pr["raw"][2 * i + w])
                        g.free = [d]
                        fin.append(d)
                    qk_ready[(b, hp)] = fin
                    if i == 3:
                        r.free = [p]
                    yield

            def attend(b, hp, sums):
                hf = hp // 4
                mt, f = Mr.take()
                sa_, sb_ = SB[hp % 2], SB[2]
                parts = [(sa_, 0, 5, 480), (sb_, 5, 8, 256)]
                for k, j0, j1, n in parts:
                    pe(mm(k.buf[:, 0:n], identb[:, :], maskb[:, 0:n], True, False, skip_group_check=True), c3, c4, k.after)
                p = None
                for odd in range(2):
                    for k, j0, j1, n in parts:
                        for j in range(j0 + (j0 + odd) % 2, j1, 2):
                            o, nq = 96 * (j - j0), min(96, L - 64 * j)
                            for s in range(2):
                                r0, r1 = 64 * s, 64 * ((s + j) % 2)
                                t = pe(mm(k.buf[r1:r1 + 64, o:o + nq], K[r0:r0 + 64, hp, 64 * j:64 * j + 64],
                                          Q[r0:r0 + 64, hp, 64 * j:64 * j + nq], False, False, skip_group_check=True),
                                       qk_ready[(b, hp)], p)
                    p = t
                    if not odd:
                        yield
                for k, j0, j1, n in parts:
                    c = 1 + 3 * j0
                    d = dve(i_tensor_reduce(mt.buf[:, c:c + n // 32], k.buf[:, 0:n].rearrange("p (a c) -> p a c", c=32),
                                            AX_X, ALU.max, apply_transpose=True), p, f, z1)
                st["k"][hp] = p
                own = mt.buf[:, 1:25].rearrange("p (r j u) -> p r j u", r=1, u=3)[:, :, :, 0:2].broadcast_to([128, 2, 8, 2])
                also = mt.buf[:, 0:24].rearrange("p (r j u) -> p r j u", r=1, u=3)[:, :, :, 0:1].broadcast_to([128, 2, 8, 2])
                d = [dve(i_tensor_copy(mt.buf[:, o:o + 32].rearrange("p (r j u) -> p r j u", r=2, u=2), x), d)
                     for o, x in ((32, own), (64, also))]
                yield
                g, f = G.take()
                for i in range(2):
                    o = 128 * i
                    pe(mm(g.buf[0:32, o:o + 128], knegb[:, 0:32], knegb[:, 32 + o:160 + o], True, False), c5, f)
                    p = pe(mm(g.buf[0:32, o:o + 128], mt.buf[:, 32 + 32 * i:64 + 32 * i], ident, False, True), d)
                d = dve(i_tensor_reduce(mt.buf[0:32, 32:64], g.buf[0:32, 0:256].rearrange("p (k c) -> p c k", k=8),
                                        AX_X, ALU.max), p)
                g.free = [d]
                er, f = Er.take()
                ep = pool(i_tensor_tensor(
                    er.buf[:, :].rearrange("p (a c) -> p a c", a=16),
                    mt.buf[0:32, 32:64].rearrange("p (o c) -> p o c", o=1).broadcast_to([32, 16, 32]),
                    cn("mske", 32).rearrange("p (a o) -> p a o", o=1).broadcast_to([32, 16, 32]), ALU.mult), d, f)
                mt.free = [ep]
                yield
                ej = er.buf[:, :].rearrange("p (j c) -> p j c", c=64)
                pt, f = Pr.take()
                done = []
                for k, j0, j1, n in reversed(parts):
                    whole = j1 - j0 if j1 < 8 else j1 - j0 - 1
                    main = j1 - j0 if j1 < 8 else 2
                    kj = k.buf[:, 0:480].rearrange("p (j c) -> p j c", c=96)
                    pe(mm(kj[:, 0:main, 0:64], nselr[:, 0:128], ej[:, j0:j0 + main, :], False, False, skip_group_check=True),
                       ep, c1)
                    if main < j1 - j0:
                        pe(mm(k.buf[:, 192:256], nselr[:, 0:128], ej[:, 7, :], False, False, skip_group_check=True))
                    p = pe(mm(kj[:, 0:whole, 64:96], nselr[:, 128:256], ej[:, j0 + 1:j0 + 1 + whole, 0:32], False, True,
                              skip_group_check=True))
                    a = act(i_activation(pt.buf[:, 96 * j0:96 * j0 + n], k.buf[:, 0:n], ACT.Exp), p, f)
                    k.after = [a]
                    done.append(a)
                er.free = [p]
                yield
                f_y = yb.free
                p = None
                for odd in range(2):
                    for j in range(odd, 8, 2):
                        nq = min(96, L - 64 * j)
                        for s in range(2):
                            r0, r1 = 64 * s, 64 * ((s + j) % 2)
                            c = 2 * (j // 2) if s == 0 else min(2 * ((j + 1) // 2) + 1, 8)
                            t = pe(mm(yb.buf[r0:r0 + 64, 64 * j:64 * j + nq], Vj[r1:r1 + 64, c, hp, :],
                                      pt.buf[r1:r1 + 64, 96 * j:96 * j + nq], j == 0, j == 7, skip_group_check=True),
                                   done, v_ready[(b, hf)], f_y, p)
                    p = t
                    if not odd:
                        yield
                st["v"][hf] = p
                t_y = act(i_copy(AO[:, hp, :], yb.buf[:, :]), p, st["ao"][hf])
                yb.free = [t_y]
                sums["pt"].append(pt)
                sums["y"].append(t_y)
                if hp % 4 == 3:
                    f = smb.free
                    for i, corner in ((0, 0), (1, 0), (0, 1), (1, 1)):
                        for c, pt in enumerate(sums["pt"]):
                            o = smb.buf[32 * c:32 * c + 32, :].rearrange("p (j c) -> p j c", c=32)
                            sel = cn("ssel")[:, 32 * i:32 * i + 32]
                            if corner:
                                n = 4 - i
                                q0 = 2 + 2 * i
                                x = pt.buf[:, 0:672].rearrange("p (j c) -> p j c", c=96)[:, i:7:2, 64:96]
                                y = o[:, q0:q0 + 4 * (n - 1) + 1:4, :]
                            elif i == 0:
                                x = pt.buf[:, 0:672].rearrange("p (j c) -> p j c", c=96)[:, 0:7:2, 0:64]
                                y = smb.buf[32 * c:32 * c + 32, :].rearrange("p (j c) -> p j c", c=64)[:, 0:8:2, :]
                            else:
                                x = pt.buf[:, 96:736].rearrange("p (j c) -> p j c", c=64)
                                y = smb.buf[32 * c:32 * c + 32, :].rearrange("p (j c) -> p j c", c=64)[:, 1:8:2, :]
                                x = x[:, 0:10:3, :]
                            p = pe(mm(y, sel, x, i == 0 and corner == 0, i == 1 and corner == 1, skip_group_check=True), f, done)
                    for pt in sums["pt"]:
                        pt.free = [p]
                    sums["p"] = p
                yield

            def scale_out(b, hf, sums):
                r, t = yield from inverses(smb, sums["p"])
                yield
                ready = []
                for i in range(4):
                    hp = 4 * hf + i
                    g, p = pair_rows(r, i, t)
                    d = dve(i_tensor_tensor(AO[:, hp, :], AO[:, hp, :], g.buf[:, :], ALU.mult), p, sums["y"][i])
                    g.free = [d]
                    ready.append(d)
                    if i == 3:
                        r.free = [p]
                    yield
                g, f = G.take()
                for i in range(4):
                    p = pe(mm(g.buf[:, :], WO[:, 4 * hf + i, :], AO[:, 4 * hf + i, :], i == 0, i == 3), ready[i], t_w["o"], f)
                st["ao"][hf] = p
                x0, x1 = X[0:64, b, 0:L], X[64:128, b, 1:1 + L]
                d1 = dve(i_tensor_tensor(x0, g.buf[0:64, :], x0, ALU.add), p, xs_of[b][1])
                d2 = dve(i_tensor_tensor(x1, g.buf[64:128, :], x1, ALU.add), p, xs_of[b][1])
                g.free = [d1, d2]
                wo_done[:] = [p]
                yield
                if hf == 1:
                    x_ready[b] = [d1, d2]
                    t = yield from variance(VAR[:, 0, 4 * b:4 * b + 4], X[:, b, 0:L], [d1, d2], var_free)
                    var_ready.append(t)

            var_ready, var_free = [], st.get("var")
            halves = [(b, hf) for b in range(NB) for hf in range(2)]
            between = ["p", "", "m", "apo", "apv",
                       "p", "o", "v", "aamp", "apo",
                       "p", "m", "v", "aapo", "aapo",
                       "v", "op", "o", "aapox", "opo"]
            tail = None
            before = None
            SB = phase_slots()
            xsplit(0)
            pr = {"adds": [], "raw": []}
            now = proj(0, 0, pr)
            vp = vproj(0, 0)
            for _ in range(8):
                steps(now)
                steps(vp)
                add(pr, 3)
            steps(now, 4)
            for n, (b, hf) in enumerate(halves):
                nxt = halves[n + 1] if n + 1 < len(halves) else None
                pr = {"adds": [], "raw": []}
                gens = {"o": tail, "m": now, "p": proj(*nxt, pr) if nxt else None, "v": vproj(*nxt) if nxt else None}
                sums = {"pt": [], "y": []}

                def fill(what):
                    for c in what:
                        if c == "x":
                            if hf == 0 and b + 1 < NB:
                                xsplit(b + 1)
                        elif c == "a":
                            add(pr, 2)
                        elif gens[c]:
                            steps(gens[c])

                for i in range(4):
                    g = attend(b, 4 * hf + i, sums)
                    part = between[5 * i:5 * i + 5]
                    steps(g)
                    fill(part[0])
                    steps(g)
                    if before:
                        steps(before)
                    fill(part[1])
                    if before:
                        steps(before, 2)
                    fill(part[2])
                    steps(g)
                    fill(part[3])
                    steps(g)
                    fill(part[4])
                    before = g
                run(*[gens[c] for c in "ov" if gens[c]])
                now = gens["p"]
                tail = scale_out(b, hf, sums)
            steps(before, 3)
            run(tail)
            end_slots(SB)
            wh_done = wq_reads[-2:]

            q.phase += 1
            t_r = rsqrt(VAR, 32, var_ready)
            var_reads = []

            def ffn(b):
                g, f = G.take()
                p = pe(mm(g.buf[:, :], cmt, X[:, b, 0:L]), x_ready[b], f)
                xc, f = Tr.take()
                t = act(i_copy(xc.buf[:, :], g.buf[:, :]), p, f)
                g.free = [t]
                g, p = spread(VAR[:, 3, 4 * b:4 * b + 4], t_r)
                var_reads.append(p)
                t = dve(i_tensor_tensor(xc.buf[:, :], xc.buf[:, :], g.buf[:, :], ALU.mult), t, p)
                g.free = [t]
                t = dve(i_tensor_scalar(xc.buf[:, :], xc.buf[:, :], VEC[:, layer, 0:1], VEC[:, layer, 1:2],
                                        ALU.mult, ALU.add), t, t_v)
                xs, f = Xr.take()
                t_xs = split(pool, xs.buf[0][:, 64:], xs.buf[1][:, 64:], xc.buf[:, :], t, f)
                xc.free = t_xs
                xh, xl = (z[:, 64:] for z in xs.buf)
                yield
                hs = []
                for i, (o, n) in enumerate(FP):
                    ga, f = G.take()
                    pa = mm3(ga.buf[0:n, :], W1H[:, o:o + n], W1L[:, o:o + n], xh, xl, t_xs, t_w["1"], f)
                    gg, f = G.take()
                    o += F1
                    pg = mm3(gg.buf[0:n, :], W1H[:, o:o + n], W1L[:, o:o + n], xh, xl, f)
                    h, f = Tr.take()
                    a = act(i_activation(h.buf[0:n, :], gg.buf[0:n, :], ACT.Gelu, bias=VEC[0:n, layer, 5 + i:6 + i]), pg, f)
                    gg.free = [a]
                    d = dve(i_scalar_tensor_tensor(h.buf[0:n, :], ga.buf[0:n, :], VEC[0:n, layer, 2 + i:3 + i],
                                                   h.buf[0:n, :], ALU.add, ALU.mult), pa, a)
                    ga.free = [d]
                    hs.append((h, d))
                    yield
                xs.free = [pg]
                w1_reads.append(pg)
                g, f = S.take()
                for i, (o, n) in enumerate(FP):
                    p = pe(mm(g.buf[:, :], W2[0:n, i, :], hs[i][0].buf[0:n, :], i == 0, i == 2), hs[i][1], t_w["2"], f)
                for h, _ in hs:
                    h.free = [p]
                x0, x1 = X[0:64, b, 0:L], X[64:128, b, 1:1 + L]
                d1 = dve(i_scalar_tensor_tensor(x0, g.buf[0:64, :], VEC[0:64, layer, 8:9], x0, ALU.add, ALU.add), p)
                d2 = dve(i_scalar_tensor_tensor(x1, g.buf[64:128, :], VEC[64:128, layer, 8:9], x1, ALU.add, ALU.add), p)
                g.free = [d1, d2]
                x_ready[b] = [d1, d2]
                w2_reads.append(p)
                yield

            w1_reads, w2_reads = [], []
            more = layer + 1 < DEPTH
            if more:
                load_wo(layer + 1)
            loader = load_split(layer + 1, st["v"]) if more else None
            gens = [ffn(b) for b in range(NB)]
            live = [gens.pop(0)]
            n = 0
            while live:
                for g in list(live):
                    if not steps(g):
                        live.remove(g)
                if loader:
                    steps(loader)
                n += 1
                if gens and len(live) < 2 and n >= 3:
                    live.append(gens.pop(0))
            if more:
                run(loader)
                w12_done = [w1_reads[-1], w2_reads[-1]]
                finish_w1(layer + 1)
            st["var"] = var_reads

        q.phase += 1
        outs = []
        act(lambda e: e.preload_act_table_set("natural_log_exp_and_others"))

        def final(b):
            u, f = Tr.take()
            a1 = act(i_copy(u.buf[0:64, :], X[0:64, b, 0:L]), x_ready[b], f)
            a2 = act(i_copy(u.buf[64:128, :], X[64:128, b, 1:1 + L]), x_ready[b])
            r, f = Tr.take()
            t_r = dma(r.buf[:, :], x1d[:, b, :], f"x{b % 2}", x1_store[b], f)
            yield
            xc, gr, t = yield from norm(u.buf[:, :], [a1, a2])
            m = dve(i_tensor_tensor(xc.buf[:, :], xc.buf[:, :], gr.buf[:, :], ALU.mult), t)
            gr.free = [m]
            m = pool(i_tensor_tensor(r.buf[:, :], r.buf[:, :], xc.buf[:, :], ALU.add), m, t_r)
            xc.free = [m]
            yield
            g, f = G.take()
            for i in range(4):
                p = pe(i_transpose(g.buf[:, 128 * i:128 * i + 128], r.buf[:, 128 * i:128 * i + 128], ident), m, f)
            a = act(i_copy(u.buf[:, :], g.buf[:, :]), p)
            g.free = [a]
            r.free = [p]
            t = dma(out[b].rearrange("(a p) d -> p a d", p=128), u.buf[:, :].rearrange("p (a d) -> p a d", a=4), f"o{b}", a)
            u.free = [t]
            outs.append(t)
            yield

        for b in range(0, NB, 2):
            run(final(b), final(b + 1))
        op("sp", None, outs, x1_store)

        q.number(lambda n: ctx.enter_context(nc.semaphore(n)))
        block = ctx.enter_context(nc.Block())

        @block.sync
        def _(e):
            q.emit("sp", e)

        @block.tensor
        def _(e):
            q.emit("pe", e)

        @block.vector
        def _(e):
            q.emit("dve", e)

        @block.scalar
        def _(e):
            q.emit("act", e)

        @block.gpsimd
        def _(e):
            q.emit("pool", e)


def kernel(**inputs):
    import numpy as _np
    import concourse.bacc as _bacc
    from concourse import mybir as _mybir
    from concourse.bass_utils import run_bass_kernel_spmd as _run

    g = {k: _np.asarray(v) for k, v in inputs.items()}
    vec = _np.zeros((128, DEPTH, 16), _np.float32)
    for l in range(DEPTH):
        vec[:, l, 0] = g["L0_ffn_ln_g"][l]
        vec[:, l, 1] = g["L0_ffn_ln_b"][l]
        for i, (o, n) in enumerate(FP):
            vec[0:n, l, 2 + i] = g["L0_ffn_b1"][l, o:o + n]
            vec[0:n, l, 5 + i] = g["L0_ffn_b1"][l, F1 + o:F1 + o + n]
        vec[:, l, 8] = g["L0_ffn_b2"][l]
        for i, n in enumerate(("L0_ffn_q_scale", "L0_ffn_k_scale")):
            s = g[n][l]
            for h in range(2):
                vec[64 * h:64 * h + 64, l, 9 + i] = s
        for h in range(2):
            vec[64 * h:64 * h + 64, l, 13] = g["L0_attn_g_weight"]
    wo = _np.ascontiguousarray(g["L0_attn_Wo"].T.reshape(8, 128, 128).transpose(1, 0, 2).reshape(128, 1024))
    data = [
        ("x", g["L0_attn_hidden_states"]), ("cst", constants()),
        ("awq", g["L0_attn_Wq"].T), ("awk", g["L0_attn_Wk"].T), ("awv", g["L0_attn_Wv"].T), ("awo", wo),
        ("wqkv", g["L0_ffn_Wqkv"]), ("wo", g["L0_ffn_Wo"]), ("w1", g["L0_ffn_W1"]), ("w2", g["L0_ffn_W2"]), ("vec", vec),
    ]
    nc = _bacc.Bacc("TRN2", target_bir_lowering=False, num_devices=1)
    arrays, args = {}, []
    for name, a in data:
        a = _np.ascontiguousarray(a)
        arrays["in_" + name] = a
        args.append(nc.dram_tensor("in_" + name, a.shape, _mybir.dt.from_np(a.dtype), kind="ExternalInput").ap())
    o = nc.dram_tensor("out_0", (NB, L, D), F32, kind="ExternalOutput").ap()
    build(nc, *args, o)
    r = _run(nc, [arrays], core_ids=[0])
    return r.results[0]["out_0"]
```
